# Optimizing a Trainium2 kernel written in Bass

```python
import numpy as np
import jax
import jax.numpy as jnp

def _softmax(x, axis=-1):
    return jax.nn.softmax(x, axis=axis)

def _gelu(x):
    return jax.nn.gelu(x, approximate=True)

def _silu(x):
    return jax.nn.silu(x)

def _sigmoid(x):
    return jax.nn.sigmoid(x)

def _layernorm(x, axis=-1, eps=1e-05):
    m = jnp.mean(x, axis=axis, keepdims=True)
    v = jnp.var(x, axis=axis, keepdims=True)
    return (x - m) / jnp.sqrt(v + eps)

def _scatter_add(tgt, idx, src, axis=0):
    return tgt.at[idx].add(src)

def _segment_sum(src, seg, n):
    return jax.ops.segment_sum(src, seg, n)
kernel_name = 'mk_perceiver_d1_seqx_r2_258c3a'

def setup_inputs(seed: int=0):
    np.random.seed(seed)
    _w = jnp.asarray

    def _rec_inputs():
        import jax
        import jax.numpy as jnp
        _rk = jax.random.key(seed)
        x = 7.22e-05 + 1 * jax.random.normal(jax.random.fold_in(_rk, 1), (16, 64, 512), jnp.float32)
        _lenS = 64 - jax.random.randint(jax.random.fold_in(_rk, 7), (16,), 0, max(1, 64 // 4) + 1, jnp.int32)
        _lenS2 = 1601 - jax.random.randint(jax.random.fold_in(_rk, 8), (16,), 0, max(1, 1601 // 4) + 1, jnp.int32)
        _ctx_1024P = jax.random.normal(jax.random.fold_in(_rk, 11), (16, 16, 512), jnp.float32)
        _ctx_1024c = jax.random.dirichlet(jax.random.fold_in(_rk, 511), 0.3 * jnp.ones((16,), jnp.float32), (16, 1601))
        _ctx_1024t = jnp.einsum('bsk,bkd->bsd', _ctx_1024c, _ctx_1024P)
        _ctx_1024t = _ctx_1024t * jax.lax.rsqrt(jnp.mean(jnp.square(_ctx_1024t)) + 1e-12) * 0.953939
        ctx_1024 = 4.13588e-05 + 0.999923 * (_ctx_1024t + 0.3 * jax.random.normal(jax.random.fold_in(_rk, 611), (16, 1601, 512), jnp.float32))
        _validS = jnp.arange(64)[None, :] < _lenS[:, None]
        _validS2 = jnp.arange(1601)[None, :] < _lenS2[:, None]
        _causal = jnp.tril(jnp.ones((64, 64), dtype=bool))
        mask_BxSxS2_ik1 = jnp.where(jnp.broadcast_to(_validS2[:, None, :], (16, 64, 1601)), 1, 0).astype(jnp.int32)
        return (x, ctx_1024, mask_BxSxS2_ik1)
    x, ctx_1024, mask_BxSxS2_ik1 = _rec_inputs()

    def _L0_xattn_setup():
        import jax, jax.numpy as jnp
        import numpy as np
        NEG = -9000000000000000.0
        EPS = 1e-05
        key = jax.random.key(seed)
        k1, k2, k3, k4 = jax.random.split(key, 4)
        B, S, D = (4, 1024, 512)
        q = jax.random.normal(k1, (B, S, D), dtype=jnp.float32)
        k = jax.random.normal(k2, (B, S, D), dtype=jnp.float32)
        v = jax.random.normal(k3, (B, S, D), dtype=jnp.float32)
        mask = jax.random.randint(k4, (B, S, S), 0, 2, dtype=jnp.int32)
        gamma = jnp.ones((D,), dtype=jnp.float32)
        beta = jnp.zeros((D,), dtype=jnp.float32)
        return {'q': q, 'k': k, 'v': v, 'mask': mask, 'gamma': gamma, 'beta': beta}
    _L0_xattn_all = _L0_xattn_setup()
    _L0_xattn_in = {k: v for k, v in _L0_xattn_all.items() if k in ('gamma', 'beta')}
    del _L0_xattn_all

    def _L0_attn_setup():
        import jax, jax.numpy as jnp
        import numpy as np
        B, S, H = (8, 1024, 512)
        key = jax.random.key(seed)
        k1, k2, k3 = jax.random.split(key, 3)
        x = jax.random.normal(k1, (B, S, H), dtype=jnp.float32)
        W_qkv = jax.random.normal(k2, (3 * H, H), dtype=jnp.float32) / np.sqrt(H)
        W_out = jax.random.normal(k3, (H, H), dtype=jnp.float32) / np.sqrt(H)
        return {'x': x, 'W_qkv': W_qkv, 'W_out': W_out}
    _L0_attn_all = _L0_attn_setup()
    _L0_attn_in = {k: v for k, v in _L0_attn_all.items() if k in ('W_qkv', 'W_out')}
    del _L0_attn_all

    def _L0_ffn_setup():
        import jax, jax.numpy as jnp
        import numpy as np
        HIDDEN = 512
        NUM_EXPERTS = 8
        TOP_K = 2
        FFN = 2048
        BATCH, SEQ = (4, 1024)
        key = jax.random.key(seed)
        k_x, k_r, k_w1, k_w2 = jax.random.split(key, 4)
        x = jax.random.normal(k_x, (BATCH, SEQ, HIDDEN), dtype=jnp.float32)
        router_w = jax.random.normal(k_r, (NUM_EXPERTS, HIDDEN), dtype=jnp.float32) * (1.0 / np.sqrt(HIDDEN))
        lim = float(np.sqrt(6.0 / (FFN + HIDDEN)))
        expert_w1 = jax.random.uniform(k_w1, (NUM_EXPERTS, FFN, HIDDEN), dtype=jnp.float32, minval=-lim, maxval=lim)
        expert_w2 = jax.random.uniform(k_w2, (NUM_EXPERTS, HIDDEN, FFN), dtype=jnp.float32, minval=-lim, maxval=lim)
        return {'x': x, 'router_w': router_w, 'expert_w1': expert_w1, 'expert_w2': expert_w2}
    _L0_ffn_all = _L0_ffn_setup()
    _L0_ffn_in = {k: v for k, v in _L0_ffn_all.items() if k in ('router_w', 'expert_w1', 'expert_w2')}
    del _L0_ffn_all
    return {'x': x, 'ctx_1024': ctx_1024, 'mask_BxSxS2_ik1': mask_BxSxS2_ik1, 'L0_xattn_gamma': _L0_xattn_in['gamma'], 'L0_xattn_beta': _L0_xattn_in['beta'], 'L0_attn_W_qkv': _L0_attn_in['W_qkv'], 'L0_attn_W_out': _L0_attn_in['W_out'], 'L0_ffn_router_w': _L0_ffn_in['router_w'], 'L0_ffn_expert_w1': _L0_ffn_in['expert_w1'], 'L0_ffn_expert_w2': _L0_ffn_in['expert_w2']}

def reference(x, ctx_1024, mask_BxSxS2_ik1, L0_xattn_gamma, L0_xattn_beta, L0_attn_W_qkv, L0_attn_W_out, L0_ffn_router_w, L0_ffn_expert_w1, L0_ffn_expert_w2):
    import jax
    import jax.numpy as jnp

    def _L0_xattn_ref(q, k, v, mask, gamma, beta):
        import jax, jax.numpy as jnp
        import numpy as np
        NEG = -9000000000000000.0
        EPS = 1e-05
        d_k = q.shape[-1]
        logits = jnp.einsum('bsd,btd->bst', q, k) / jnp.sqrt(jnp.asarray(d_k, q.dtype))
        logits = jnp.where(mask == 0, jnp.asarray(NEG, logits.dtype), logits)
        attn = jax.nn.softmax(logits, axis=-1)
        x = jnp.einsum('bst,btd->bsd', attn, v)
        mu = jnp.mean(x, axis=-1, keepdims=True)
        var = jnp.mean(jnp.square(x - mu), axis=-1, keepdims=True)
        xhat = (x - mu) * jax.lax.rsqrt(var + EPS)
        return xhat * gamma + beta

    def _L0_attn_ref(x, W_qkv, W_out):
        import jax, jax.numpy as jnp
        import numpy as np
        B, S, H = (8, 1024, 512)
        h = x.shape[-1]
        scale = 1.0 / np.sqrt(h).astype(np.float32)
        y = jnp.einsum('bsh,oh->bso', x, W_qkv).reshape(*x.shape, 3)
        q, k, v = (y[..., 0], y[..., 1], y[..., 2])
        scores = jnp.einsum('bqh,bkh->bqk', q, k) * scale
        attn = jax.nn.softmax(scores, axis=-1)
        ctx = jnp.einsum('bqk,bkh->bqh', attn, v)
        out = jnp.einsum('bsh,oh->bso', ctx, W_out)
        return out

    def _L0_ffn_ref(x, router_w, expert_w1, expert_w2):
        import jax, jax.numpy as jnp
        import numpy as np
        HIDDEN = 512
        NUM_EXPERTS = 8
        TOP_K = 2
        FFN = 2048
        BATCH, SEQ = (4, 1024)
        B, S, D = x.shape
        xf = x.reshape(-1, D)
        scores = xf @ router_w.T
        top_v, top_i = jax.lax.top_k(scores, TOP_K)
        routing_w = jax.nn.softmax(top_v, axis=-1)
        out = jnp.zeros_like(xf)
        for e in range(NUM_EXPERTS):
            w_e = jnp.sum(jnp.where(top_i == e, routing_w, 0.0), axis=-1)
            h = jax.nn.gelu(xf @ expert_w1[e].T, approximate=False)
            out = out + h @ expert_w2[e].T * w_e[:, None]
        return out.reshape(B, S, D)
    x = x + _L0_xattn_ref(_layernorm(x, axis=-1), ctx_1024, ctx_1024, mask_BxSxS2_ik1, L0_xattn_gamma, L0_xattn_beta)
    x = x + _L0_attn_ref(_layernorm(x, axis=-1), L0_attn_W_qkv, L0_attn_W_out)
    x = x + _L0_ffn_ref(_layernorm(x, axis=-1), L0_ffn_router_w, L0_ffn_expert_w1, L0_ffn_expert_w2)
    return x

_drawn_inputs = setup_inputs


def setup_inputs(seed=0):
    import zlib

    import numpy as np

    out = dict(_drawn_inputs(seed))
    spreads = {'L0_xattn_gamma': (1.0, 0.2), 'L0_xattn_beta': (0.0, 0.1)}
    factors = {}
    for name, (base, spread) in spreads.items():
        noise = np.random.default_rng([zlib.crc32(name.encode()), seed]).standard_normal(out[name].shape)
        drawn = base * np.exp(spread * noise) if base else spread * noise
        out[name] = jnp.asarray(drawn.astype(out[name].dtype))
    for name, factor in factors.items():
        out[name] = (out[name] * factor).astype(out[name].dtype)
    return out
```

```python
from contextlib import ExitStack

import concourse.bass as bass
from concourse import mybir

ALU = mybir.AluOpType
ACT = mybir.ActivationFunctionType
AX = mybir.AxisListType
F32 = mybir.dt.float32
I32 = mybir.dt.int32

P = 128
BATCH, SEQ, D = 16, 64, 512
T = 1601
TILES = BATCH * SEQ // P
KC = D // P
BLK = 512
CHUNKS = -(-T // P)
T_REST = T - (CHUNKS - 1) * P
NBLK = -(-T // BLK)
EXPERTS, FFN = 8, 2048
FB = FFN // BLK
FC = FFN // P
TOP_K = 2
SLOTS = (TOP_K * TILES * P + EXPERTS * (P - 1)) // P
SCALE = float(D) ** -0.5
EPS = 1e-5
MASKED = -9000000000000000.0
LIMIT = 2.0 ** 53
HUGE = 3.0e38
GUESS = float(0x5F3759DF)
NEWTON = 3

C_ID, C_TRI, C_ONE, C_EXP, C_SLOT = 0, P, 2 * P, 3 * P, 3 * P + TILES * EXPERTS
C_END = C_SLOT + SLOTS * EXPERTS

FILLS_BLK = [2 * KC] * (NBLK - 1) + [2]
FIRST_FILL = [1 + sum(FILLS_BLK[:n]) for n in range(NBLK)]
QK_FILLS = 1 + sum(FILLS_BLK)
P_FILLS = -(-CHUNKS // 4)
FILLS = QK_FILLS + P_FILLS
BANKS = 3


def by_act(r):
    return r % 2 == 0


def upto(r, act):
    return sum(by_act(x) == act for x in range(r + 1))


def count_at(j, r, n_qk, n_all, n_r):
    if isinstance(j, int) and j == -1:
        return n_r
    if isinstance(j, int) and j == TILES - 1:
        return n_all * j + n_r
    return j * n_all + (n_qk + n_r)


def filled_at(j, r):
    return count_at(j, r, QK_FILLS, FILLS, r + 1)


def copied_at(j, r):
    act = by_act(r)
    return act, count_at(j, r, upto(QK_FILLS - 1, act), upto(FILLS - 1, act), upto(r, act))


def bank_before(j, r):
    last = isinstance(j, int) and j == TILES - 1
    if r >= BANKS and not (last and r < QK_FILLS + BANKS):
        return j, r - BANKS
    if isinstance(j, int) and j == -1:
        return None
    top = QK_FILLS if isinstance(j, int) and j == 0 else FILLS
    return j - 1, max(x for x in range(top) if x % BANKS == r % BANKS)


class Steps:

    def __init__(self, engine, semaphore):
        self.engine, self.semaphore, self.before, self.n = engine, semaphore, 0, 0

    def then_next(self, instruction):
        instruction.then_inc(self.semaphore, 1)
        self.n += 1
        self.engine.wait_ge(self.semaphore, self.before + self.n)

    def enter(self, turn, per_turn):
        self.start = self.before + self.n
        self.before, self.n, self.per_turn = turn * per_turn + self.start, 0, per_turn

    def leave(self, turns):
        assert self.n == self.per_turn, self.n
        self.before, self.n = self.start + turns * self.per_turn, 0


def build(nc, x, ctx_in, mask, gamma, beta, w_qkv, w_out, w_router, w1, w2, consts, out):
    slots_x = nc.dram_tensor("slots_x", (SLOTS * P, D), F32, kind="Internal").ap()
    slots_y = nc.dram_tensor("slots_y", (SLOTS * P, D), F32, kind="Internal").ap()

    with ExitStack() as stack:
        def sb(name, shape, dt=F32):
            return stack.enter_context(nc.sbuf_tensor(name, shape, dt))

        def sem(name):
            return stack.enter_context(nc.semaphore(name))

        res = sb("res", [P, TILES * D])
        cst = sb("cst", [P, C_END])
        small = sb("small", [P, 64])
        route = sb("route", [P, 1100])
        arena = sb("arena", [P, 44358])

        def view(at, *dims):
            n = 1
            for d in dims:
                n *= d
            a = arena[:, at:at + n]
            if len(dims) == 2:
                a = a.rearrange("p (a b) -> p a b", a=dims[0])
            if len(dims) == 3:
                a = a.rearrange("p (a b c) -> p a b c", a=dims[0], b=dims[1])
            return a

        ident = cst[:, C_ID:C_ID + P]
        before_me = cst[:, C_TRI:C_TRI + P]
        ones = cst[:, C_ONE:C_ONE + P]
        expert_no = cst[:, C_EXP:C_SLOT].rearrange("p (t e) -> p t e", e=EXPERTS)
        slot_row = cst[:, C_SLOT:C_END].rearrange("p (s e) -> p s e", e=EXPERTS)

        ctxb = [view(i * 2 * CHUNKS * D, 2, CHUNKS, D) for i in range(2)]
        ctxT = [view(26624 + i * 4096, 2, KC, BLK) for i in range(2)]
        mask_sb = arena[:, 34816:34816 + T].bitcast(I32)
        bound = arena[:, 36418:36418 + T]
        prob = arena[:, 38020:38020 + T]
        probT = view(39622, CHUNKS, P)
        xqT = [view(41286 + i * D, KC, P) for i in range(2)]
        xq = arena[:, 42310:42310 + D]
        att = arena[:, 42822:42822 + D]
        gam = arena[:, 43334:43334 + D]
        bet = arena[:, 43846:43846 + D]
        wqkv_sb = view(0, 3, KC, D)
        wo_sb = view(6144, KC, D)
        rw_sb = view(8192, KC, EXPERTS)
        zeros = arena[:, 8224:8224 + D]
        xn = [arena[:, 26624 + i * D:26624 + (i + 1) * D] for i in range(2)]
        xnT = [view(27648 + i * D, KC, P) for i in range(2)]
        qT = [view(28672 + i * D, KC, P) for i in range(2)]
        kT = [view(29696 + i * D, KC, P) for i in range(2)]
        vv = [arena[:, 30720 + i * D:30720 + (i + 1) * D] for i in range(2)]
        pr = [arena[:, 31744 + i * P:31744 + (i + 1) * P] for i in range(2)]
        prT = arena[:, 32000:32000 + P]
        cT = view(32128, KC, P)
        xn2T = view(32640, KC, P)
        xr = arena[:, 33152:33152 + D]
        xn2 = arena[:, 34816:34816 + TILES * D]
        w1b = [view(i * 16384, FB, KC, BLK) for i in range(2)]
        w2b = [view(8192 + i * 16384, FC, D) for i in range(2)]
        xg = [arena[:, 32768 + i * D:32768 + (i + 1) * D] for i in range(2)]
        xgT = [view(33792 + i * D, KC, P) for i in range(2)]
        hid = arena[:, 38912:38912 + FFN]
        hidT = view(40960, FC, P)
        yb = [arena[:, 43008 + i * D:43008 + (i + 1) * D] for i in range(2)]
        ya = [arena[:, 16384 + (2 * t) * D:16384 + (2 * t + 1) * D] for t in range(TILES)]
        yc = [arena[:, 16384 + (2 * t + 1) * D:16384 + (2 * t + 2) * D] for t in range(TILES)]

        stats, mv, rstd = small[:, 0:6], small[:, 6:8], small[:, 8:9]
        var, half = small[:, 9:10], small[:, 18:19]
        top, negtop = small[:, 10:11], small[:, 12:14]
        rowsum, inv = small[:, 14:16], small[:, 16:17]

        NTE = TILES * EXPERTS

        def rt(at, *dims):
            n = 1
            for d in dims:
                n *= d
            a = route[:, at:at + n]
            return a.rearrange("p (a b) -> p a b", a=dims[0]) if len(dims) == 2 else a

        logit = rt(0, TILES, EXPERTS)
        pick = [rt(NTE * (1 + i), TILES, EXPERTS) for i in range(2)]
        tmp = rt(NTE * 3, TILES, EXPERTS)
        logit2 = rt(NTE * 4, TILES, EXPERTS)
        both = rt(NTE * 5, TILES, EXPERTS)
        cum = rt(NTE * 6, TILES + 1, EXPERTS)
        posn = rt(NTE * 7 + 8, TILES, EXPERTS)
        scr = NTE * 8 + 8
        best = [rt(scr + 8 * i, TILES) for i in range(2)]
        low = rt(scr + 16, TILES)
        ratio = rt(scr + 24, TILES)
        gate = [rt(scr + 32 + 8 * i, TILES) for i in range(2)]
        posf = rt(scr + 48, TILES)
        pos = [rt(scr + 56 + 8 * i, TILES).bitcast(I32) for i in range(2)]
        cnt_i = rt(scr + 72, EXPERTS).bitcast(I32)
        cnt_r = rt(scr + 80, EXPERTS).bitcast(I32)
        rows = rt(scr + 88, EXPERTS)
        base = rt(scr + 96, EXPERTS + 1)
        slot_cmp = rt(scr + 112, SLOTS, EXPERTS)
        slot_f = rt(scr + 112 + SLOTS * EXPERTS, SLOTS)
        slot_e = rt(scr + 136 + SLOTS * EXPERTS, SLOTS).bitcast(I32)

        ps = stack.enter_context(nc.psum_tensor("ps", [P, 8 * BLK], F32))

        def bank(i, n=1):
            return ps[:, i * BLK:(i + n) * BLK]

        x_in, cst_in, gb_in = sem("x_in"), sem("cst_in"), sem("gb_in")
        ctx_here = [[sem(f"ctx_here{i}_{b}") for b in range(NBLK)] for i in range(2)]
        mask_in = sem("mask_in")
        a_own, v_own, p_own = sem("a_own"), sem("v_own"), sem("p_own")
        xq_ready = sem("xq_ready")
        filled = sem("filled")
        copied = {True: sem("copied_by_act"), False: sem("copied_by_dve")}
        scored = sem("scored")
        bound_ready = sem("bound_ready")
        masked = sem("masked")
        negtop_ready = sem("negtop_ready")
        exp_done = sem("exp_done")
        pv_done = sem("pv_done")
        att_read = sem("att_read")
        att_ready = sem("att_ready")
        res1 = sem("res1")

        w_in, zero_set, zero_out = sem("w_in"), sem("zero_set"), sem("zero_out")
        pr_clear = sem("pr_clear")
        xn_ready = sem("xn_ready")
        t1_done, t1_copied = sem("t1_done"), sem("t1_copied")
        q_done, q_copied = sem("q_done"), sem("q_copied")
        k_done, k_copied = sem("k_done"), sem("k_copied")
        v_done, v_copied = sem("v_done"), sem("v_copied")
        s_done, top_ready, e_done, pr_ready = sem("s_done"), sem("top_ready"), sem("e_done"), sem("pr_ready")
        pt_done, pt_copied = sem("pt_done"), sem("pt_copied")
        ct_done, ct_copied = sem("ct_done"), sem("ct_copied")
        o_done, res2 = sem("o_done"), sem("res2")
        xn2_ready = sem("xn2_ready")
        t2_done, t2_copied = sem("t2_done"), sem("t2_copied")
        r_done, r_copied = sem("r_done"), sem("r_copied")

        best_ready, ratio_ready = sem("best_ready"), sem("ratio_ready")
        cum_ready, rank_done = sem("cum_ready"), sem("rank_done")
        pos_ready, slot_ready, scattered = sem("pos_ready"), sem("slot_ready"), sem("scattered")

        x_here = [sem(f"x_here{i}") for i in range(2)]
        w1_here = [sem(f"w1_here{i}") for i in range(2)]
        w2_here = [sem(f"w2_here{i}") for i in range(2)]
        x_turned, x_copied = sem("x_turned"), sem("x_copied")
        up_done, gelu_done = sem("up_done"), sem("gelu_done")
        h_turned, h_copied = sem("h_turned"), sem("h_copied")
        down_done, y_ready = sem("down_done"), sem("y_ready")
        y_out = [sem(f"y_out{i}") for i in range(2)]
        gathered = [sem(f"gathered{t}") for t in range(TILES)]
        sum_ready, stored = sem("sum_ready"), sem("stored")

        block = stack.enter_context(nc.Block())

        def tile_of(j):
            return res[:, bass.ds(j * D, D)]

        def apart(engine):
            if engine is nc.vector:
                engine.memset(small[:, 20:21], 0.0)
            else:
                engine.tensor_tensor(small[:, 22:23], small[:, 21:22], small[:, 21:22], ALU.add)

        def place(eng, j, p, par, r):
            o = bank(NBLK + r % BANKS)
            copy = eng.copy if by_act(r) else eng.tensor_copy
            if r == 0:
                return eng.mul(xqT[par], o.rearrange("p (k t) -> p k t", k=KC), SCALE)
            if r >= QK_FILLS:
                c = 4 * (r - QK_FILLS)
                if r < QK_FILLS + 2 and not (isinstance(j, int) and j == 0):
                    eng.wait_ge(pv_done, j)
                if c + 4 <= CHUNKS:
                    return copy(probT[:, c:c + 4, :], o.rearrange("p (c q) -> p c q", c=4))
                return copy(probT[0:T_REST, c, :], o[0:T_REST, 0:P])
            blk = max(b for b in range(NBLK) if FIRST_FILL[b] <= r)
            n = r - FIRST_FILL[blk]
            if n < 2 and not (isinstance(p, int) and p == 0 and blk < 2):
                eng.wait_ge(scored, p * NBLK + (blk - 1))
            if blk < NBLK - 1:
                return copy(ctxT[blk % 2][:, n // KC, n % KC, :], o)
            return copy(ctxT[blk % 2][:, n, :, 0:T_REST], o.rearrange("p (k t) -> p k t", k=KC)[:, :, 0:T_REST])

        @block.sync
        def _(sp):
            def load_ctx(p, h, par):
                for blk in range(NBLK):
                    for b in range(2):
                        src = ctx_in[bass.ds(2 * p + b, 1), :, :]
                        if blk < NBLK - 1:
                            sp.dma_start(ctxb[par][:, b, 4 * blk:4 * blk + 4, :],
                                         src[:, blk * BLK:(blk + 1) * BLK, :].rearrange("o (c p) d -> p (o c) d", p=P)
                                         ).then_inc(ctx_here[par][blk], 16)
                        else:
                            sp.dma_start(ctxb[par][0:T_REST, b, CHUNKS - 1, :],
                                         src[:, (CHUNKS - 1) * P:T, :].rearrange("o p d -> p (o d)")
                                         ).then_inc(ctx_here[par][blk], 16)

            def load_mask(p):
                sp.dma_start(mask_sb, mask[bass.ds(p * P, P), :]).then_inc(mask_in, 16)

            sp.dma_start(cst[:], consts).then_inc(cst_in, 16)
            sp.dma_start(res[:].rearrange("p (t d) -> p t d", d=D),
                         x.rearrange("(t p) d -> p t d", p=P)).then_inc(x_in, 16)
            load_ctx(0, 0, 0)
            load_mask(0)
            sp.dma_start(gam, gamma.partition_broadcast(P)).then_inc(gb_in, 16)
            sp.dma_start(bet, beta.partition_broadcast(P)).then_inc(gb_in, 16)
            load_ctx(1, 0, 1)
            sp.wait_ge(bound_ready, 1)
            load_mask(1)
            with sp.Fori(1, TILES // 2) as h:
                for par in range(2):
                    p = h * 2 + par
                    sp.wait_ge(pv_done, p - 1)
                    load_ctx(p, h, par)
                    sp.wait_ge(bound_ready, p)
                    load_mask(p)
            sp.wait_ge(pv_done, TILES - 1)
            sp.dma_start(wqkv_sb, w_qkv.rearrange("p (j k h) -> p j k h", j=3, k=KC)).then_inc(w_in, 16)
            sp.dma_start(wo_sb, w_out.rearrange("p (k h) -> p k h", k=KC)).then_inc(w_in, 16)
            sp.dma_start(rw_sb, w_router.rearrange("p (k e) -> p k e", k=KC)).then_inc(w_in, 16)
            sp.wait_ge(zero_set, 1)
            sp.dma_start(slots_x.rearrange("(s p) d -> p s d", p=P),
                         zeros.unsqueeze(1).to_broadcast([P, SLOTS, D])).then_inc(zero_out, 16)

            def load_x(i, par):
                sp.dma_start(xg[par], slots_x[bass.ds(i * P, P), :]).then_inc(x_here[par], 16)

            sp.wait_ge(scattered, 16 * TOP_K * TILES)
            load_x(0, 0)
            load_x(1, 1)
            with sp.Fori(1, SLOTS // 2) as h:
                for par in range(2):
                    sp.wait_ge(x_turned, h * 2 + (par - 1))
                    load_x(h * 2 + par, par)
            for i in range(SLOTS // 2 * 2, SLOTS):
                sp.wait_ge(x_turned, i - 1)
                load_x(i, i % 2)
            for t in range(TILES):
                sp.wait_ge(sum_ready, t + 1)
                sp.dma_start(out[t * P:(t + 1) * P, :], res[:, t * D:(t + 1) * D]).then_inc(stored, 16)
            sp.wait_ge(stored, 16 * TILES)

        @block.gpsimd
        def _(pool):
            own = Steps(pool, p_own)

            def bounds(p):
                pool.wait_ge(mask_in, p * 16 + 16)
                if not (isinstance(p, int) and p == 0):
                    pool.wait_ge(masked, p * 2)
                apart(pool)
                pool.tensor_scalar(bound, mask_sb, 0, MASKED - LIMIT, ALU.is_equal, ALU.mult).then_inc(bound_ready, 1)

            def residual(j):
                pool.wait_ge(att_ready, j + 1)
                own.then_next(pool.tensor_tensor(att, att, gam, ALU.mult))
                own.then_next(pool.tensor_tensor(att, att, bet, ALU.add))
                pool.tensor_tensor(tile_of(j), tile_of(j), att, ALU.add).then_inc(res1, 1)

            own.then_next(pool.memset(small[:, 21:22], 0.0))
            bounds(0)
            bounds(1)
            pool.wait_ge(gb_in, 32)
            with pool.Fori(0, TILES - 2) as j:
                own.enter(j, 2)
                bounds(j + 2)
                residual(j)
                own.leave(TILES - 2)
            residual(TILES - 2)
            residual(TILES - 1)

            pool.wait_ge(zero_out, 16)
            pool.wait_ge(pos_ready, 2)
            pool.wait_ge(xn2_ready, TILES)
            for t in range(TILES):
                for n in range(TOP_K):
                    pool.indirect_dma_start(
                        out=slots_x, out_offset=bass.IndirectOffsetOnAxis(ap=pos[n][:, t:t + 1], axis=0),
                        in_=xn2[:, t * D:(t + 1) * D], in_offset=None).then_inc(scattered, 16)
            pool.wait_ge(y_out[0], 16 * ((SLOTS + 1) // 2))
            pool.wait_ge(y_out[1], 16 * (SLOTS // 2))
            pool.wait_ge(down_done, SLOTS)
            for t in range(TILES):
                for n, y in enumerate((ya[t], yc[t])):
                    pool.indirect_dma_start(
                        out=y, out_offset=None, in_=slots_y,
                        in_offset=bass.IndirectOffsetOnAxis(ap=pos[n][:, t:t + 1], axis=0)).then_inc(gathered[t], 16)

        @block.tensor
        def _(pe):
            tp = [bank(NBLK + n) for n in range(BANKS)]
            att_ps = bank(7)

            def open_fill(j, r):
                if (prev := bank_before(j, r)) is not None:
                    act, n = copied_at(*prev)
                    pe.wait_ge(copied[act], n)
                return tp[r % BANKS]

            def scores(p, par, j, blk):
                n = min(BLK, T - blk * BLK)
                last = FIRST_FILL[blk] + FILLS_BLK[blk] - 1
                for r in (last - 1, last):
                    act, count = copied_at(j, r)
                    pe.wait_ge(copied[act], count)
                if blk == 0 and not (isinstance(p, int) and p == 0):
                    pe.wait_ge(masked, p * 2)
                for k in range(KC):
                    for b in range(2):
                        mm = pe.matmul(ps[64 * b:64 * b + 64, blk * BLK:blk * BLK + n],
                                       xqT[par][:, k, 64 * b:64 * b + 64], ctxT[blk % 2][:, b, k, 0:n],
                                       start=(k == 0), stop=(k == KC - 1))
                mm.then_inc(scored, 1)

            def qk(p, h, par, j):
                pe.wait_ge(xq_ready, p + 1)
                o = open_fill(j, 0)
                for k in range(KC):
                    mm = pe.transpose(o[:, k * P:(k + 1) * P], xq[:, k * P:(k + 1) * P], ident)
                mm.then_inc(filled, 1)
                for blk in range(NBLK):
                    pe.wait_ge(ctx_here[par][blk], h * 32 + 32)
                    r = FIRST_FILL[blk]
                    for b in range(2):
                        if blk < NBLK - 1:
                            for k in range(KC):
                                o = open_fill(j, r)
                                for c in range(4):
                                    mm = pe.transpose(o[:, c * P:(c + 1) * P],
                                                      ctxb[par][:, b, 4 * blk + c, k * P:(k + 1) * P], ident)
                                mm.then_inc(filled, 1)
                                r += 1
                        else:
                            o = open_fill(j, r)
                            for k in range(KC):
                                mm = pe.transpose(o[:, k * P:k * P + T_REST],
                                                  ctxb[par][0:T_REST, b, CHUNKS - 1, k * P:(k + 1) * P],
                                                  ident[0:T_REST, 0:T_REST])
                            mm.then_inc(filled, 1)
                            r += 1
                    if blk:
                        scores(p, par, j, blk - 1)
                scores(p, par, j, NBLK - 1)

            def pv(j, par):
                pe.wait_ge(exp_done, j + 1)
                for n in range(P_FILLS):
                    o = open_fill(j, QK_FILLS + n)
                    for c in range(4 * n, min(4 * n + 4, CHUNKS)):
                        m = P if c < CHUNKS - 1 else T_REST
                        mm = pe.transpose(o[0:m, (c % 4) * P:(c % 4 + 1) * P], prob[:, c * P:c * P + m], ident)
                    mm.then_inc(filled, 1)
                if not (isinstance(j, int) and j == 0):
                    pe.wait_ge(att_read, j)
                for c in range(CHUNKS):
                    m = P if c < CHUNKS - 1 else T_REST
                    if c % 4 == 0:
                        act, count = copied_at(j, QK_FILLS + c // 4)
                        pe.wait_ge(copied[act], count)
                    for b in range(2):
                        mm = pe.matmul(att_ps[64 * b:64 * b + 64, :], probT[0:m, c, 64 * b:64 * b + 64],
                                       ctxb[par][0:m, b, c, :], start=(c == 0), stop=(c == CHUNKS - 1))
                mm.then_inc(pv_done, 1)

            pe.wait_ge(cst_in, 16)
            qk(0, 0, 0, -1)
            qk(1, 0, 1, 0)
            pv(0, 0)
            with pe.Fori(0, TILES // 2 - 1) as h:
                for par in range(2):
                    j = h * 2 + (1 + par)
                    qk(j + 1, h + 1, par, j)
                    pv(j, 1 - par)
            pv(TILES - 1, 1)

            S, TB, QB, KB, VB, MB, CB, OB = (bank(n) for n in range(8))

            def turn_first(j, par):
                pe.wait_ge(xn_ready, j + 1)
                for k in range(KC):
                    mm = pe.transpose(TB[:, k * P:(k + 1) * P], xn[par][:, k * P:(k + 1) * P], ident)
                mm.then_inc(t1_done, 1)

            def project(j, par, which, dst, copied_out, done):
                pe.wait_ge(t1_copied, j + 1)
                if not isinstance(j, int) or j >= 1:
                    pe.wait_ge(copied_out, j)
                for hc in range(KC):
                    for k in range(KC):
                        mm = pe.matmul(dst[:, hc * P:(hc + 1) * P], wqkv_sb[:, which, k, hc * P:(hc + 1) * P],
                                       xnT[par][:, k, :], start=(k == 0), stop=(k == KC - 1))
                mm.then_inc(done, 1)

            def values(j, par):
                if not isinstance(j, int) or j >= 1:
                    pe.wait_ge(v_copied, j)
                for k in range(KC):
                    mm = pe.matmul(VB, xnT[par][:, k, :], wqkv_sb[:, 2, k, :], start=(k == 0), stop=(k == KC - 1))
                mm.then_inc(v_done, 1)

            def own_scores(j, par):
                pe.wait_ge(q_copied, j + 1)
                pe.wait_ge(k_copied, j + 1)
                if not isinstance(j, int) or j >= 1:
                    pe.wait_ge(e_done, j)
                for k in range(KC):
                    mm = pe.matmul(S[:, 0:P], qT[par][:, k, :], kT[par][:, k, :], start=(k == 0), stop=(k == KC - 1))
                mm.then_inc(s_done, 1)

            def turn_probs(j, par):
                pe.wait_ge(pr_ready, j + 1)
                pe.transpose(MB[:, 0:P], pr[par], ident).then_inc(pt_done, 1)

            def weigh(j, par):
                pe.wait_ge(pt_copied, j + 1)
                pe.wait_ge(v_copied, j + 1)
                if not isinstance(j, int) or j >= 1:
                    pe.wait_ge(ct_copied, j)
                for hc in range(KC):
                    mm = pe.matmul(CB[:, hc * P:(hc + 1) * P], vv[par][:, hc * P:(hc + 1) * P], prT,
                                   start=True, stop=True)
                mm.then_inc(ct_done, 1)

            def project_out(j):
                pe.wait_ge(ct_copied, j + 1)
                if not isinstance(j, int) or j >= 1:
                    pe.wait_ge(res2, j)
                for hc in range(KC):
                    mm = pe.matmul(OB, cT[:, hc, :], wo_sb[:, hc, :], start=(hc == 0), stop=(hc == KC - 1))
                mm.then_inc(o_done, 1)

            def turn_second(j, first):
                pe.wait_ge(xn2_ready, j + 1)
                pe.wait_ge(t1_copied, first)
                for k in range(KC):
                    mm = pe.transpose(TB[:, k * P:(k + 1) * P], xr[:, k * P:(k + 1) * P], ident)
                mm.then_inc(t2_done, 1)

            def router(j):
                pe.wait_ge(t2_copied, j + 1)
                for k in range(KC):
                    mm = pe.matmul(MB[:, P:P + EXPERTS], xn2T[:, k, :], rw_sb[:, k, :],
                                   start=(k == 0), stop=(k == KC - 1))
                mm.then_inc(r_done, 1)

            def tile_step(j, par, front, back):
                own_scores(j, par)
                if front:
                    turn_first(j + 1, 1 - par)
                    project(j + 1, 1 - par, 0, QB, q_copied, q_done)
                if back:
                    turn_second(j - 1, j + 2 if front else TILES)
                turn_probs(j, par)
                if front:
                    project(j + 1, 1 - par, 1, KB, k_copied, k_done)
                weigh(j, par)
                if back:
                    router(j - 1)
                if front:
                    values(j + 1, 1 - par)
                project_out(j)

            pe.wait_ge(w_in, 48)
            pe.wait_ge(att_read, TILES)
            turn_first(0, 0)
            project(0, 0, 0, QB, q_copied, q_done)
            project(0, 0, 1, KB, k_copied, k_done)
            values(0, 0)
            tile_step(0, 0, True, False)
            with pe.Fori(0, TILES // 2 - 1) as h:
                for par in range(2):
                    tile_step(h * 2 + (1 + par), 1 - par, True, True)
            tile_step(TILES - 1, 1, False, True)
            turn_second(TILES - 1, TILES)
            router(TILES - 1)

            pe.wait_ge(cum_ready, 1)
            pe.matmul(bank(0)[:, 0:NTE], before_me, both.rearrange("p t e -> p (t e)"), start=True, stop=False)
            pe.matmul(bank(0)[:, 0:NTE], ones, cum[:, 0:TILES, :].rearrange("p t e -> p (t e)"), start=False, stop=True)
            pe.matmul(bank(1)[:, 0:EXPERTS], ones, cum[:, TILES, :], start=True, stop=True).then_inc(rank_done, 1)

            UB, HB, YB, XB = [bank(0), bank(1), bank(2)], [bank(3), bank(4)], [bank(5), bank(6)], bank(7)

            def turn_x(i, h, par):
                pe.wait_ge(x_here[par], h * 16 + 16)
                if not isinstance(i, int) or i >= 1:
                    pe.wait_ge(x_copied, i)
                for k in range(KC):
                    mm = pe.transpose(XB[:, k * P:(k + 1) * P], xg[par][:, k * P:(k + 1) * P], ident)
                mm.then_inc(x_turned, 1)

            def up(i, par, f):
                if not (isinstance(i, int) and i == 0 and f < 3):
                    pe.wait_ge(gelu_done, i * FB + (f - 2))
                for k in range(KC):
                    mm = pe.matmul(UB[f % 3], xgT[par][:, k, :], w1b[par][:, f, k, :], start=(k == 0), stop=(k == KC - 1))
                mm.then_inc(up_done, 1)

            def turn_h(i, f):
                pe.wait_ge(gelu_done, i * FB + (f + 1))
                if not (isinstance(i, int) and i == 0 and f < 2):
                    pe.wait_ge(h_copied, i * FB + (f - 1))
                for c in range(4):
                    mm = pe.transpose(HB[f % 2][:, c * P:(c + 1) * P], hid[:, f * BLK + c * P:f * BLK + (c + 1) * P], ident)
                mm.then_inc(h_turned, 1)

            def down(i, par, f):
                pe.wait_ge(h_copied, i * FB + (f + 1))
                for c in range(4 * f, 4 * f + 4):
                    mm = pe.matmul(YB[par], hidT[:, c, :], w2b[par][:, c, :], start=(c == 0), stop=(c == FC - 1))
                if f == FB - 1:
                    mm.then_inc(down_done, 1)

            def slot(i, h, par, last=False):
                pe.wait_ge(x_copied, i + 1)
                pe.wait_ge(w1_here[par], h * 16 + 16)
                up(i, par, 0)
                up(i, par, 1)
                turn_h(i, 0)
                up(i, par, 2)
                turn_h(i, 1)
                up(i, par, 3)
                turn_h(i, 2)
                pe.wait_ge(w2_here[par], h * 16 + 16)
                if not isinstance(i, int) or i >= 2:
                    pe.wait_ge(y_ready, i - 1)
                down(i, par, 0)
                down(i, par, 1)
                turn_h(i, 3)
                if not last:
                    turn_x(i + 1, h + par, 1 - par)
                down(i, par, 2)
                down(i, par, 3)

            turn_x(0, 0, 0)
            slot(0, 0, 0)
            slot(1, 0, 1)
            with pe.Fori(1, SLOTS // 2) as h:
                for par in range(2):
                    slot(h * 2 + par, h, par)
            slot(SLOTS - 1, SLOTS // 2, 0, last=True)

        @block.scalar
        def _(act):
            def copy_out(j, p, par, r):
                act.wait_ge(filled, filled_at(j, r))
                place(act, j, p, par, r).then_inc(copied[True], 1)

            def qk_copies(j, p, par):
                for r in range(QK_FILLS):
                    if by_act(r):
                        copy_out(j, p, par, r)

            def exps(j, par):
                act.wait_ge(negtop_ready, j + 1)
                nc.scalar.activation(prob, prob, ACT.Exp, bias=negtop[:, par:par + 1], scale=1.0,
                                     accum_out=rowsum[:, par:par + 1]).then_inc(exp_done, 1)

            def p_copies(j):
                for r in range(QK_FILLS, FILLS):
                    if by_act(r):
                        copy_out(j, j, 0, r)

            act.wait_ge(cst_in, 16)
            qk_copies(-1, 0, 0)
            exps(0, 0)
            qk_copies(0, 1, 1)
            p_copies(0)
            with act.Fori(0, TILES // 2 - 1) as h:
                for par in range(2):
                    j = h * 2 + (1 + par)
                    exps(j, 1 - par)
                    qk_copies(j, j + 1, par)
                    p_copies(j)
            exps(TILES - 1, 1)
            p_copies(TILES - 1)

            def copy_t1(j, par):
                act.wait_ge(t1_done, j + 1)
                if not isinstance(j, int) or j >= 2:
                    act.wait_ge(v_done, j - 1)
                act.copy(xnT[par], bank(1).rearrange("p (k t) -> p k t", k=KC)).then_inc(t1_copied, 1)

            def copy_qkv(j, par):
                for n, (done, copied_out, dst) in enumerate(((q_done, q_copied, qT), (k_done, k_copied, kT),
                                                             (v_done, v_copied, vv))):
                    act.wait_ge(done, j + 1)
                    if not isinstance(j, int) or j >= 2:
                        act.wait_ge(s_done if n < 2 else ct_done, j - 1)
                    src = bank(2 + n)
                    if n < 2:
                        src = src.rearrange("p (k t) -> p k t", k=KC)
                    act.copy(dst[par], src).then_inc(copied_out, 1)

            def own_exps(j, par):
                act.wait_ge(top_ready, j + 1)
                for b in range(2):
                    q = slice(64 * b, 64 * b + 64)
                    e = nc.scalar.activation(pr[par][q, 64 * b:64 * b + 64], bank(0)[q, 64 * b:64 * b + 64], ACT.Exp,
                                             bias=negtop[q, par:par + 1], scale=SCALE,
                                             accum_out=rowsum[q, par:par + 1])
                e.then_inc(e_done, 1)

            copy_t1(0, 0)
            copy_qkv(0, 0)
            act.wait_ge(pr_clear, 2)
            copy_t1(1, 1)
            own_exps(0, 0)
            copy_qkv(1, 1)
            with act.Fori(0, TILES // 2 - 1) as h:
                for par in range(2):
                    j = h * 2 + (1 + par)
                    copy_t1(j + 1, par)
                    own_exps(j, 1 - par)
                    copy_qkv(j + 1, par)
            own_exps(TILES - 1, 1)

            act.wait_ge(best_ready, 1)
            nc.scalar.activation(ratio, ratio, ACT.Exp).then_inc(ratio_ready, 1)

            def load_w1(e, par):
                act.dma_start(w1b[par], w1[bass.ds(e, 1), :, :].rearrange("o p (f k n) -> p (o f) k n", f=FB, k=KC)
                              ).then_inc(w1_here[par], 16)

            def load_w2(e, par):
                act.dma_start(w2b[par], w2[bass.ds(e, 1), :, :].rearrange("o p (c n) -> p (o c) n", c=FC)
                              ).then_inc(w2_here[par], 16)

            def expert(i):
                return act.value_load(slot_e[0:1, bass.ds(i, 1)], min_val=0, max_val=EXPERTS - 1)

            def gelus(i):
                for f in range(FB):
                    act.wait_ge(up_done, i * FB + (f + 1))
                    if not (isinstance(i, int) and i == 0):
                        act.wait_ge(h_turned, i * FB + (f - FB + 1))
                    nc.scalar.activation(hid[:, f * BLK:(f + 1) * BLK], bank(f % 3), ACT.Gelu).then_inc(gelu_done, 1)

            def store_y(i, par):
                act.wait_ge(y_ready, i + 1)
                act.dma_start(slots_y[bass.ds(i * P, P), :], yb[par]).then_inc(y_out[par], 16)

            act.wait_ge(zero_out, 16)
            act.wait_ge(slot_ready, 1)
            for i in range(2):
                e = expert(i)
                load_w1(e, i)
                load_w2(e, i)
            gelus(0)
            e = expert(2)
            load_w1(e, 0)
            with act.Fori(0, (SLOTS - 3) // 2) as h:
                for par in range(2):
                    i = h * 2 + par
                    store_y(i, par)
                    e = expert(i + 2)
                    load_w2(e, par)
                    gelus(i + 1)
                    e = expert(i + 3)
                    load_w1(e, 1 - par)
            for i in range(SLOTS - 3, SLOTS):
                store_y(i, i % 2)
                if i + 2 < SLOTS:
                    load_w2(expert(i + 2), i % 2)
                if i + 1 < SLOTS:
                    gelus(i + 1)
                if i + 3 < SLOTS:
                    load_w1(expert(i + 3), (i + 1) % 2)

        @block.vector
        def _(dve):
            own = Steps(dve, v_own)

            def rsqrt(v, variance):
                own.then_next(dve.tensor_scalar(v, variance, EPS, None, ALU.add))
                own.then_next(dve.tensor_scalar(rstd.bitcast(I32), v.bitcast(I32), -0.5, GUESS, ALU.mult, ALU.add))
                for _ in range(NEWTON):
                    own.then_next(dve.scalar_tensor_tensor(out=half, in0=rstd, scalar=rstd, in1=v,
                                                           op0=ALU.mult, op1=ALU.mult))
                    own.then_next(dve.tensor_scalar(half, half, -0.5, 1.5, ALU.mult, ALU.add))
                    own.then_next(dve.tensor_tensor(rstd, rstd, half, ALU.mult))

            NORM = 2 + 2 + 3 * NEWTON

            def normalize(dst, src):
                apart(nc.vector)
                own.then_next(dve.bn_stats(stats, src))
                apart(nc.vector)
                own.then_next(dve.bn_aggr(mv, stats))
                rsqrt(var, mv[:, 1:2])
                return dve.tensor_scalar(dst, src, mv[:, 0:1], rstd, ALU.subtract, ALU.mult)

            def queries(p):
                if not isinstance(p, int) or p >= 1:
                    dve.wait_ge(filled, filled_at(p - 2 if not isinstance(p, int) or p > 1 else -1, 0))
                normalize(xq, tile_of(p)).then_inc(xq_ready, 1)

            def softmax(j, par):
                dve.wait_ge(bound_ready, j + 1)
                if not isinstance(j, int) or j >= 1:
                    dve.wait_ge(filled, filled_at(j - 1, FILLS - 1))
                for n, (a, b) in enumerate(((0, 2 * BLK), (2 * BLK, T))):
                    dve.wait_ge(scored, j * NBLK + (2 * n + 2))
                    dve.scalar_tensor_tensor(out=prob[:, a:b], in0=bound[:, a:b], scalar=LIMIT, in1=ps[:, a:b],
                                             op0=ALU.add, op1=ALU.min).then_inc(masked, 1)
                dve.wait_ge(masked, j * 2 + 2)
                own.then_next(dve.tensor_reduce(top, prob, AX.X, ALU.max))
                dve.tensor_scalar(negtop[:, par:par + 1], top, -1.0, None, ALU.mult).then_inc(negtop_ready, 1)

            def attended(j, par):
                dve.wait_ge(pv_done, j + 1)
                own.then_next(dve.reciprocal(inv, rowsum[:, par:par + 1]))
                if not isinstance(j, int) or j >= 1:
                    dve.wait_ge(res1, j)
                dve.tensor_scalar(att, bank(7), inv, None, ALU.mult).then_inc(att_read, 1)
                dve.wait_ge(att_read, j + 1)
                normalize(att, att).then_inc(att_ready, 1)

            def copies(j, p, par, rs):
                for r in rs:
                    if not by_act(r):
                        dve.wait_ge(filled, filled_at(j, r))
                        place(dve, j, p, par, r).then_inc(copied[False], 1)

            dve.wait_ge(x_in, 16)
            queries(0)
            copies(-1, 0, 0, range(QK_FILLS))
            queries(1)
            softmax(0, 0)
            copies(0, 1, 1, range(FILLS))
            with dve.Fori(0, TILES // 2 - 1) as h:
                own.enter(h, 2 * (NORM + 1 + 1 + NORM))
                for par in range(2):
                    j = h * 2 + (1 + par)
                    queries(j + 1)
                    softmax(j, 1 - par)
                    copies(j, j + 1, par, range(FIRST_FILL[1]))
                    attended(j - 1, par)
                    copies(j, j + 1, par, range(FIRST_FILL[1], FILLS))
                own.leave(TILES // 2 - 1)
            softmax(TILES - 1, 1)
            attended(TILES - 2, 0)
            copies(TILES - 1, TILES - 1, 1, range(QK_FILLS, FILLS))
            attended(TILES - 1, 1)

            def first_norm(j, par):
                dve.wait_ge(res1, j + 1)
                if not isinstance(j, int) or j >= 2:
                    dve.wait_ge(t1_done, j - 1)
                normalize(xn[par], tile_of(j)).then_inc(xn_ready, 1)

            def tops(j, par):
                dve.wait_ge(s_done, j + 1)
                for b in range(2):
                    q = slice(64 * b, 64 * b + 64)
                    own.then_next(dve.tensor_reduce(top[q, :], bank(0)[q, 64 * b:64 * b + 64], AX.X, ALU.max))
                dve.tensor_scalar(negtop[:, par:par + 1], top, -SCALE, None, ALU.mult).then_inc(top_ready, 1)

            def probs(j, par):
                dve.wait_ge(e_done, j + 1)
                own.then_next(dve.reciprocal(inv, rowsum[:, par:par + 1]))
                dve.tensor_scalar(pr[par], pr[par], inv, None, ALU.mult).then_inc(pr_ready, 1)

            def copy_pt(j):
                dve.wait_ge(pt_done, j + 1)
                if not isinstance(j, int) or j >= 1:
                    dve.wait_ge(ct_done, j)
                dve.tensor_copy(prT, bank(5)[:, 0:P]).then_inc(pt_copied, 1)

            def copy_ct(j):
                dve.wait_ge(ct_done, j + 1)
                if not isinstance(j, int) or j >= 1:
                    dve.wait_ge(o_done, j)
                dve.tensor_copy(cT, bank(6).rearrange("p (k t) -> p k t", k=KC)).then_inc(ct_copied, 1)

            def copy_t2(j):
                dve.wait_ge(t2_done, j + 1)
                if not isinstance(j, int) or j >= 1:
                    dve.wait_ge(r_done, j)
                dve.tensor_copy(xn2T, bank(1).rearrange("p (k t) -> p k t", k=KC)).then_inc(t2_copied, 1)

            def copy_router(j):
                dve.wait_ge(r_done, j + 1)
                dve.tensor_copy(route[:, bass.ds(j * EXPERTS, EXPERTS)], bank(5)[:, P:P + EXPERTS]).then_inc(r_copied, 1)

            def second_norm(j):
                dve.wait_ge(o_done, j + 1)
                dve.tensor_tensor(tile_of(j), bank(7), tile_of(j), ALU.add).then_inc(res2, 1)
                dve.wait_ge(res2, j + 1)
                if not isinstance(j, int) or j >= 1:
                    dve.wait_ge(t2_done, j)
                own.then_next(normalize(xr, tile_of(j)))
                dve.tensor_copy(xn2[:, bass.ds(j * D, D)], xr).then_inc(xn2_ready, 1)

            def tile_step(j, par, front, back):
                tops(j, par)
                if front:
                    first_norm(j + 2, par)
                probs(j, par)
                if back:
                    copy_t2(j - 1)
                copy_pt(j)
                copy_ct(j)
                if back:
                    copy_router(j - 1)
                second_norm(j)

            dve.memset(zeros, 0.0).then_inc(zero_set, 1)
            for i in range(2):
                dve.memset(pr[i], 0.0).then_inc(pr_clear, 1)
            first_norm(0, 0)
            first_norm(1, 1)
            tile_step(0, 0, True, False)
            with dve.Fori(0, (TILES - 4) // 2) as h:
                own.enter(h, 2 * (2 + NORM + 1 + NORM + 1))
                for par in range(2):
                    tile_step(h * 2 + (1 + par), 1 - par, True, True)
                own.leave((TILES - 4) // 2)
            for j in range(TILES - 3, TILES):
                tile_step(j, j % 2, j + 2 < TILES, True)
            copy_t2(TILES - 1)
            copy_router(TILES - 1)
            dve.wait_ge(r_copied, TILES)

            def spread(a, n=EXPERTS):
                return a.unsqueeze(2).to_broadcast([P, TILES, n])

            src = logit
            for n in range(TOP_K):
                own.then_next(dve.tensor_reduce(best[n], src, AX.X, ALU.max))
                own.then_next(dve.tensor_tensor(tmp, src, spread(best[n]), ALU.is_equal))
                own.then_next(dve.scalar_tensor_tensor(out=tmp, in0=tmp, scalar=-100.0, in1=expert_no,
                                                       op0=ALU.mult, op1=ALU.add))
                own.then_next(dve.tensor_reduce(low, tmp, AX.X, ALU.min))
                own.then_next(dve.tensor_tensor(pick[n], tmp, spread(low), ALU.is_equal))
                if n == 0:
                    own.then_next(dve.scalar_tensor_tensor(out=logit2, in0=pick[0], scalar=-HUGE, in1=logit,
                                                           op0=ALU.mult, op1=ALU.add))
                    src = logit2
            dve.tensor_tensor(ratio, best[1], best[0], ALU.subtract).then_inc(best_ready, 1)
            own.then_next(dve.memset(cum[:, 0, :], 0.0))
            own.then_next(dve.tensor_tensor(both, pick[0], pick[1], ALU.add))
            for t in range(TILES):
                last = dve.tensor_tensor(cum[:, t + 1, :], cum[:, t, :], both[:, t, :], ALU.add)
                if t < TILES - 1:
                    own.then_next(last)
            last.then_inc(cum_ready, 1)
            dve.wait_ge(ratio_ready, 1)
            own.then_next(dve.tensor_scalar(low, ratio, 1.0, None, ALU.add))
            own.then_next(dve.reciprocal(gate[0], low))
            own.then_next(dve.tensor_tensor(gate[1], ratio, gate[0], ALU.mult))
            dve.wait_ge(rank_done, 1)
            own.then_next(dve.tensor_scalar(cnt_i, bank(1)[:, 0:EXPERTS], float(P - 1), None, ALU.add))
            own.then_next(dve.tensor_scalar(cnt_r, cnt_i, 7, 7, ALU.logical_shift_right, ALU.logical_shift_left))
            own.then_next(dve.tensor_copy(rows, cnt_r))
            own.then_next(dve.memset(base[:, 0:1], 0.0))
            for e in range(EXPERTS):
                own.then_next(dve.tensor_tensor(base[:, e + 1:e + 2], base[:, e:e + 1], rows[:, e:e + 1], ALU.add))
            own.then_next(dve.tensor_tensor(slot_cmp, slot_row,
                                            base[:, 1:].unsqueeze(1).to_broadcast([P, SLOTS, EXPERTS]), ALU.is_ge))
            own.then_next(dve.tensor_reduce(slot_f, slot_cmp, AX.X, ALU.add))
            dve.tensor_scalar(slot_e, slot_f, float(EXPERTS - 1), None, ALU.min).then_inc(slot_ready, 1)
            own.then_next(dve.tensor_tensor(posn, bank(0)[:, 0:NTE].rearrange("p (t e) -> p t e", e=EXPERTS),
                                            base[:, 0:EXPERTS].unsqueeze(1).to_broadcast([P, TILES, EXPERTS]), ALU.add))
            for n in range(TOP_K):
                own.then_next(dve.tensor_tensor(tmp, pick[n], posn, ALU.mult))
                own.then_next(dve.tensor_reduce(posf, tmp, AX.X, ALU.add))
                dve.tensor_copy(pos[n], posf).then_inc(pos_ready, 1)
                dve.wait_ge(pos_ready, n + 1)

            def copy_x(i, par):
                dve.wait_ge(x_turned, i + 1)
                dve.tensor_copy(xgT[par], bank(7).rearrange("p (k t) -> p k t", k=KC)).then_inc(x_copied, 1)

            def copy_h(i, f):
                dve.wait_ge(h_turned, i * FB + (f + 1))
                if not isinstance(i, int) or i >= 1:
                    if f == 0:
                        dve.wait_ge(down_done, i)
                dve.tensor_copy(hidT[:, 4 * f:4 * f + 4, :], bank(3 + f % 2).rearrange("p (c t) -> p c t", c=4)
                                ).then_inc(h_copied, 1)

            def copy_y(i, h, par):
                dve.wait_ge(down_done, i + 1)
                if not isinstance(i, int) or i >= 2:
                    dve.wait_ge(y_out[par], h * 16)
                dve.tensor_copy(yb[par], bank(5 + par)).then_inc(y_ready, 1)

            def slot(i, h, par, last=False):
                for f in range(FB):
                    copy_h(i, f)
                if not last:
                    copy_x(i + 1, 1 - par)
                copy_y(i, h, par)

            copy_x(0, 0)
            slot(0, 0, 0)
            slot(1, 0, 1)
            with dve.Fori(1, SLOTS // 2) as h:
                for par in range(2):
                    slot(h * 2 + par, h, par)
            slot(SLOTS - 1, SLOTS // 2, 0, last=True)

            for t in range(TILES):
                dve.wait_ge(gathered[t], 32)
                own.then_next(dve.scalar_tensor_tensor(out=ya[t], in0=ya[t], scalar=gate[0][:, t:t + 1],
                                                       in1=res[:, t * D:(t + 1) * D], op0=ALU.mult, op1=ALU.add))
                dve.scalar_tensor_tensor(out=res[:, t * D:(t + 1) * D], in0=yc[t], scalar=gate[1][:, t:t + 1],
                                         in1=ya[t], op0=ALU.mult, op1=ALU.add).then_inc(sum_ready, 1)


def kernel(x, ctx_1024, mask_BxSxS2_ik1, L0_xattn_gamma, L0_xattn_beta, L0_attn_W_qkv, L0_attn_W_out,
           L0_ffn_router_w, L0_ffn_expert_w1, L0_ffn_expert_w2):
    import numpy as np
    import concourse.bacc as bacc
    from concourse.bass_utils import run_bass_kernel_spmd

    c = np.zeros((P, C_END), np.float32)
    c[:, C_ID:C_ID + P] = np.eye(P)
    c[:, C_TRI:C_TRI + P] = np.triu(np.ones((P, P)), 1)
    c[:, C_ONE:C_ONE + P] = 1.0
    c[:, C_EXP:C_SLOT] = np.tile(np.arange(EXPERTS), TILES)
    c[:, C_SLOT:C_END] = np.repeat(np.arange(SLOTS) * P, EXPERTS)
    a = {
        "x": np.asarray(x).reshape(TILES * P, D),
        "ctx": np.asarray(ctx_1024),
        "mask": np.asarray(mask_BxSxS2_ik1).reshape(TILES * P, T),
        "gamma": np.asarray(L0_xattn_gamma),
        "beta": np.asarray(L0_xattn_beta),
        "w_qkv": np.asarray(L0_attn_W_qkv).reshape(D, 3, KC, P).transpose(3, 1, 2, 0).reshape(P, -1),
        "w_out": np.asarray(L0_attn_W_out).reshape(D, KC, P).transpose(2, 1, 0).reshape(P, -1),
        "w_router": np.asarray(L0_ffn_router_w).reshape(EXPERTS, KC, P).transpose(2, 1, 0).reshape(P, -1),
        "w1": np.asarray(L0_ffn_expert_w1).reshape(EXPERTS, FB, BLK, KC, P).transpose(0, 4, 1, 3, 2)
        .reshape(EXPERTS, P, -1),
        "w2": np.asarray(L0_ffn_expert_w2).reshape(EXPERTS, D, FC, P).transpose(0, 3, 2, 1).reshape(EXPERTS, P, -1),
        "consts": c,
    }
    a = {f"in_{k}": np.ascontiguousarray(v) for k, v in a.items()}
    nc = bacc.Bacc("TRN2", target_bir_lowering=False, num_devices=1)
    args = [nc.dram_tensor(k, v.shape, mybir.dt.from_np(v.dtype), kind="ExternalInput").ap() for k, v in a.items()]
    out = nc.dram_tensor("out_0", (TILES * P, D), F32, kind="ExternalOutput").ap()
    build(nc, *args, out)
    r = run_bass_kernel_spmd(nc, [a], core_ids=[0])
    return np.asarray(r.results[0]["out_0"]).reshape(BATCH, SEQ, D)
```

```python
from contextlib import ExitStack

import concourse.bass as bass
from concourse import mybir

ALU = mybir.AluOpType
ACT = mybir.ActivationFunctionType
AX = mybir.AxisListType
F32 = mybir.dt.float32
F32R = mybir.dt.float32r
I32 = mybir.dt.int32

P = 128
BATCH, SEQ, D = 16, 64, 512
T = 1601
TILES = BATCH * SEQ // P
KC = D // P
BLK = 512
CHUNKS = -(-T // P)
T_REST = T - (CHUNKS - 1) * P
NBLK = -(-T // BLK)
EXPERTS, FFN = 8, 2048
FB = FFN // BLK
FC = FFN // P
WB, WBLK = 2 * FB, KC * BLK
TOP_K = 2
TOKENS = TILES * P
SLOTS = (TOP_K * TOKENS + EXPERTS * (P - 1)) // P
ROOM = TOKENS // P
PLACES = EXPERTS * ROOM + 1
SCALE = float(D) ** -0.5
EPS = 1e-5
MASKED = -9000000000000000.0
LIMIT = 2.0 ** 53
HUGE = 3.0e38
GUESS = float(0x5F3759DF)
NEWTON = 3

C_ID, C_TRI, C_ONE, C_ME, C_SPARE, C_EXP = 0, P, 2 * P, 3 * P, 3 * P + 1, 3 * P + 2
C_ROOM = C_EXP + EXPERTS
C_SLOT = C_ROOM + EXPERTS
C_END = C_SLOT + SLOTS * EXPERTS

LOADED_TURNED = 1
SUM_ORDER = [NBLK - 1] + list(range(LOADED_TURNED, NBLK - 1)) + list(range(LOADED_TURNED))
TURN_ORDER = [NBLK - 1] + list(range(LOADED_TURNED, NBLK - 1))
FILLS_BLK = {b: 2 * KC if b < NBLK - 1 else 2 for b in TURN_ORDER}
FIRST_FILL = {b: 1 + sum(FILLS_BLK[c] for c in TURN_ORDER[:n]) for n, b in enumerate(TURN_ORDER)}
QK_FILLS = 1 + sum(FILLS_BLK.values())
P_FILLS = -(-CHUNKS // 4)
FILLS = QK_FILLS + P_FILLS
BANKS = 3


def by_act(r):
    return r % 3 != 2


def upto(r, act):
    return sum(by_act(x) == act for x in range(r + 1))


def count_at(j, r, n_qk, n_all, n_r):
    if isinstance(j, int) and j == -1:
        return n_r
    if isinstance(j, int) and j == TILES - 1:
        return n_all * j + n_r
    return j * n_all + (n_qk + n_r)


def filled_at(j, r):
    return count_at(j, r, QK_FILLS, FILLS, r + 1)


def copied_at(j, r):
    act = by_act(r)
    return act, count_at(j, r, upto(QK_FILLS - 1, act), upto(FILLS - 1, act), upto(r, act))


def bank_before(j, r):
    last = isinstance(j, int) and j == TILES - 1
    if r >= BANKS and not (last and r < QK_FILLS + BANKS):
        return j, r - BANKS
    if isinstance(j, int) and j == -1:
        return None
    top = QK_FILLS if isinstance(j, int) and j == 0 else FILLS
    return j - 1, max(x for x in range(top) if x % BANKS == r % BANKS)


class Steps:

    def __init__(self, engine, semaphore):
        self.engine, self.semaphore, self.before, self.n = engine, semaphore, 0, 0

    def then_next(self, instruction):
        instruction.then_inc(self.semaphore, 1)
        self.n += 1
        self.engine.wait_ge(self.semaphore, self.before + self.n)

    def enter(self, turn, per_turn):
        self.start = self.before + self.n
        self.before, self.n, self.per_turn = turn * per_turn + self.start, 0, per_turn

    def leave(self, turns):
        assert self.n == self.per_turn, self.n
        self.before, self.n = self.start + turns * self.per_turn, 0


def build(nc, x, ctx_in, ctx_turned, mask, gamma, beta, w_qkv, w_out, w_router, w1, w2, consts, acc):
    tokens_x = nc.dram_tensor("tokens_x", (TOKENS + P, D), F32, kind="Internal").ap()
    slots_m = nc.dram_tensor("slots_m", (PLACES * P, 2), F32, kind="Internal").ap()

    with ExitStack() as stack:
        def sb(name, shape, dt=F32):
            return stack.enter_context(nc.sbuf_tensor(name, shape, dt))

        def sem(name):
            return stack.enter_context(nc.semaphore(name))

        res = sb("res", [P, TILES * D])
        cst = sb("cst", [P, C_END])
        small = sb("small", [P, 64])
        route = sb("route", [P, 1100])
        zeros = sb("zeros", [P, D])
        nobody = sb("nobody", [P, PLACES, 2])
        with nc.sbuf_tensor("arena", [P, 44358 + 2 * KC * T_REST], F32) as arena:
            pass
        with nc.sbuf_tensor("before_w", [P, 13312], F32), nc.sbuf_tensor("w_raw_space", [P, WB, WBLK], F32) as w_raw_space:
            pass
        low_space = sb("low_space", [P, 12288], F32R)
        rows_space = sb("rows_space", [P, 2 * D])
        w_low = sb("w_low", [P, WB, WBLK], F32R)
        h_parts = sb("h_parts", [P, 2, FC, P], F32R)
        hid = sb("hid", [P, FFN])
        yb_space = sb("yb_space", [P, 2 * D])
        sb("gap", [P, 384])
        mid_space = sb("mid_space", [P, 6144], F32R)

        def view(at, *dims):
            n = 1
            for d in dims:
                n *= d
            a = arena[:, at:at + n]
            if len(dims) == 2:
                a = a.rearrange("p (a b) -> p a b", a=dims[0])
            if len(dims) == 3:
                a = a.rearrange("p (a b c) -> p a b c", a=dims[0], b=dims[1])
            return a

        ident = cst[:, C_ID:C_ID + P]
        before_me = cst[:, C_TRI:C_TRI + P]
        ones = cst[:, C_ONE:C_ONE + P]
        me = cst[:, C_ME:C_ME + 1]
        spare = cst[:, C_SPARE:C_SPARE + 1]
        expert_no = cst[:, C_EXP:C_EXP + EXPERTS]
        room_at = cst[:, C_ROOM:C_ROOM + EXPERTS]
        slot_no = cst[:, C_SLOT:C_END].rearrange("p (s e) -> p s e", e=EXPERTS)

        ctxb = [view(i * 2 * CHUNKS * D, 2, CHUNKS, D) for i in range(2)]
        ctxT = [view(26624 + i * 4096, 2, KC, BLK) for i in range(2)]
        ctxT_rest = view(44358, 2, KC, T_REST)
        mask_sb = arena[:, 34816:34816 + T].bitcast(I32)
        bound = arena[:, 36418:36418 + T]
        prob = arena[:, 38020:38020 + T]
        probT = view(39622, CHUNKS, P)
        xqT = [view(41286 + i * D, KC, P) for i in range(2)]
        xq = arena[:, 42310:42310 + D]
        att = arena[:, 42822:42822 + D]
        gam = arena[:, 43334:43334 + D]
        bet = arena[:, 43846:43846 + D]
        wqkv_sb = view(0, 3, KC, D)
        wo_sb = view(6144, KC, D)
        rw_sb = view(12288, KC, EXPERTS)
        SELF = 29696
        xn = [arena[:, SELF + i * D:SELF + (i + 1) * D] for i in range(2)]
        xnT = [view(SELF + (2 + i) * D, KC, P) for i in range(2)]
        qT = [view(SELF + (4 + i) * D, KC, P) for i in range(2)]
        kT = [view(SELF + (6 + i) * D, KC, P) for i in range(2)]
        vv = [arena[:, SELF + (8 + i) * D:SELF + (9 + i) * D] for i in range(2)]
        xr = [arena[:, SELF + (10 + i) * D:SELF + (11 + i) * D] for i in range(2)]
        cT = view(SELF + 12 * D, KC, P)
        xrT = view(SELF + 13 * D, KC, P)
        pr = [arena[:, SELF + 14 * D + i * P:SELF + 14 * D + (i + 1) * P] for i in range(2)]
        prT = arena[:, SELF + 14 * D + 2 * P:SELF + 14 * D + 3 * P]
        xg = [rows_space[:, i * D:(i + 1) * D] for i in range(2)]
        yb = [yb_space[:, i * D:(i + 1) * D] for i in range(2)]

        def flat(tensor, at_):
            return tensor[:, at_:at_ + WBLK]

        w_raw = [w_raw_space[:, b, :] for b in range(WB)]
        w_high = ([flat(low_space, 8192 + b * WBLK) for b in range(2)] + [flat(mid_space, b * WBLK) for b in range(3)]
                  + [flat(low_space, b * WBLK) for b in range(3)])
        xT_parts = [[low_space[:, 6144 + (2 * i + part) * D:6144 + (2 * i + part + 1) * D]
                     .rearrange("p (k t) -> p k t", k=KC) for part in range(2)] for i in range(2)]

        stats, mv, rstd = small[:, 0:6], small[:, 6:8], small[:, 8:9]
        var, half = small[:, 9:10], small[:, 18:19]
        top, negtop = small[:, 10:11], small[:, 12:14]
        rowsum, inv = small[:, 14:16], small[:, 16:17]

        at = [0]

        def rt(*dims):
            n = dims[0] * (dims[1] if len(dims) == 2 else 1)
            a = route[:, at[0]:at[0] + n]
            at[0] += n
            return a.rearrange("p (a b) -> p a b", a=dims[0]) if len(dims) == 2 else a

        logit, logit2, tmp, rank = rt(EXPERTS), rt(EXPERTS), rt(EXPERTS), rt(EXPERTS)
        pick = [[rt(EXPERTS) for _ in range(TOP_K)] for _ in range(2)]
        both = [rt(EXPERTS) for _ in range(2)]
        cum = [rt(EXPERTS) for _ in range(2)]
        best, low, posf, token = rt(TOP_K), rt(1), rt(1), rt(1)
        ratio = [rt(1) for _ in range(2)]
        pos = [rt(TOP_K).bitcast(I32) for _ in range(2)]
        meta = [rt(TOP_K, 2) for _ in range(2)]
        meta_i = [m.bitcast(I32) for m in meta]
        gm = [rt(2) for _ in range(2)]
        cnt_i, cnt_r = rt(EXPERTS).bitcast(I32), rt(EXPERTS).bitcast(I32)
        lots, ends = rt(EXPERTS), rt(EXPERTS + 1)
        past, before_f, weighed = rt(SLOTS, EXPERTS), rt(SLOTS), rt(SLOTS, EXPERTS)
        taken, slot_f = rt(SLOTS), rt(SLOTS)
        slot_e, slot_at = rt(SLOTS).bitcast(I32), rt(SLOTS).bitcast(I32)

        ps = stack.enter_context(nc.psum_tensor("ps", [P, 8 * BLK], F32))

        def bank(i, n=1):
            return ps[:, i * BLK:(i + n) * BLK]

        x_in, x_rest_in, cst_in, gb_in = sem("x_in"), sem("x_rest_in"), sem("cst_in"), sem("gb_in")
        ctx_here = [[sem(f"ctx_here{i}_{b}") for b in range(NBLK)] for i in range(2)]
        ctxT_here = [sem(f"ctxT_here{b}") for b in range(LOADED_TURNED)]
        mask_in = sem("mask_in")
        a_own, v_own, p_own = sem("a_own"), sem("v_own"), sem("p_own")
        xq_ready = sem("xq_ready")
        filled = sem("filled")
        copied = {True: sem("copied_by_act"), False: sem("copied_by_dve")}
        scored = sem("scored")
        bound_ready = sem("bound_ready")
        masked = sem("masked")
        negtop_ready = sem("negtop_ready")
        exp_done = sem("exp_done")
        pv_block = sem("pv_block")
        att_read = sem("att_read")
        att_ready = sem("att_ready")
        res1 = sem("res1")

        w_in, zero_set, zero_out = sem("w_in"), sem("zero_set"), sem("zero_out")
        pr_clear = sem("pr_clear")
        xn_ready = sem("xn_ready")
        t1_done, t1_copied = sem("t1_done"), sem("t1_copied")
        q_done, q_copied = sem("q_done"), sem("q_copied")
        k_done, k_copied = sem("k_done"), sem("k_copied")
        v_done, v_copied = sem("v_done"), sem("v_copied")
        s_done, top_ready, e_done, pr_ready = sem("s_done"), sem("top_ready"), sem("e_done"), sem("pr_ready")
        pt_done, pt_copied = sem("pt_done"), sem("pt_copied")
        ct_done, ct_copied = sem("ct_done"), sem("ct_copied")
        o_done, res2 = sem("o_done"), sem("res2")
        xn2_ready = sem("xn2_ready")
        t2_done, t2_copied = sem("t2_done"), sem("t2_copied")
        r_done = sem("r_done")

        picked, ratio_ready = sem("picked"), sem("ratio_ready")
        rank_done, pos_ready = sem("rank_done"), sem("pos_ready")
        sent, acc_set = sem("sent"), sem("acc_set")
        count_done, slot_ready = sem("count_done"), sem("slot_ready")

        places_free = sem("places_free")
        x_out = [sem(f"x_out{i}") for i in range(2)]
        m_here = [sem(f"m_here{i}") for i in range(2)]
        x_here = [sem(f"x_here{i}") for i in range(2)]
        raw_here = [sem(f"raw_here{b}") for b in range(WB)]
        w_high_ready, w_ready = sem("w_high_ready"), sem("w_ready")
        x_turned, x_high_ready, x_ready = sem("x_turned"), sem("x_high_ready"), sem("x_ready")
        up_done, gelu_done = sem("up_done"), sem("gelu_done")
        h_turned, h_high_ready, h_ready = sem("h_turned"), sem("h_high_ready"), sem("h_ready")
        down_done, y_ready = sem("down_done"), sem("y_ready")
        added = [sem(f"added{i}") for i in range(2)]

        block = stack.enter_context(nc.Block())

        def load_block(eng, e, b):
            w, n = (w1, b) if b < FB else (w2, b - FB)
            eng.dma_start(w_raw[b], w[bass.ds(e, 1), :, n * WBLK:(n + 1) * WBLK].rearrange("o p n -> p (o n)")
                          ).then_inc(raw_here[b], 16)

        def tile_of(j):
            return res[:, bass.ds(j * D, D)]

        def carry_waits(dve):
            dve.memset(small[:, 20:21], 0.0)

        def carry_pool_waits(pool, own):
            pool.wait_ge(p_own, own.before + own.n)
            pool.tensor_tensor(small[:, 22:23], small[:, 21:22], small[:, 21:22], ALU.add).then_inc(p_own, 1)
            own.n += 1

        def place(eng, j, p, par, r):
            o = bank(NBLK + r % BANKS)
            copy = eng.copy if by_act(r) else eng.tensor_copy
            if r == 0:
                return eng.mul(xqT[par], o.rearrange("p (k t) -> p k t", k=KC), SCALE)
            if r >= QK_FILLS:
                c = 4 * SUM_ORDER[r - QK_FILLS]
                if r < QK_FILLS + 2 and not (isinstance(j, int) and j == 0):
                    eng.wait_ge(pv_block, j * NBLK)
                if c + 4 <= CHUNKS:
                    return copy(probT[:, c:c + 4, :], o.rearrange("p (c q) -> p c q", c=4))
                return copy(probT[0:T_REST, c, :], o[0:T_REST, 0:P])
            blk = max(TURN_ORDER, key=lambda b: FIRST_FILL[b] if FIRST_FILL[b] <= r else -1)
            n = r - FIRST_FILL[blk]
            if blk == NBLK - 1:
                if n == 0 and not (isinstance(p, int) and p == 0):
                    eng.wait_ge(scored, p * NBLK)
                return copy(ctxT_rest[:, n, :, :], o.rearrange("p (k t) -> p k t", k=KC)[:, :, 0:T_REST])
            if n < 2 and not (isinstance(p, int) and p == 0 and blk < 2):
                eng.wait_ge(scored, p * NBLK + (blk - 1))
            return copy(ctxT[blk % 2][:, n // KC, n % KC, :], o)

        @block.sync
        def _(sp):
            def load_ctx(p, par, blks=SUM_ORDER):
                for blk in blks:
                    if not (isinstance(p, int) and p < 2):
                        sp.wait_ge(pv_block, p * NBLK + (SUM_ORDER.index(blk) + 1 - 2 * NBLK))
                        if blk == 0:
                            sp.wait_ge(bound_ready, p)
                            load_mask(p)
                    for b in range(2):
                        src = ctx_in[bass.ds(2 * p + b, 1), :, :]
                        if blk < NBLK - 1:
                            sp.dma_start(ctxb[par][:, b, 4 * blk:4 * blk + 4, :],
                                         src[:, blk * BLK:(blk + 1) * BLK, :].rearrange("o (c p) d -> p (o c) d", p=P)
                                         ).then_inc(ctx_here[par][blk], 16)
                        else:
                            sp.dma_start(ctxb[par][0:T_REST, b, CHUNKS - 1, :],
                                         src[:, (CHUNKS - 1) * P:T, :].rearrange("o p d -> p (o d)")
                                         ).then_inc(ctx_here[par][blk], 16)

            def load_turned(p, blk):
                if not (isinstance(p, int) and p == 0):
                    sp.wait_ge(scored, p * NBLK - 1)
                for b in range(2):
                    sp.dma_start(ctxT[blk][:, b, :, :],
                                 ctx_turned[bass.ds(2 * p + b, 1), :, LOADED_TURNED - 1 - blk, :, :]
                                 .rearrange("o p k n -> p (o k) n")).then_inc(ctxT_here[blk], 16)

            def load_mask(p):
                sp.dma_start(mask_sb, mask[bass.ds(p * P, P), :]).then_inc(mask_in, 16)

            sp.dma_start(res[:, 0:D], x[0:P, :]).then_inc(x_in, 16)
            sp.dma_start(cst[:], consts).then_inc(cst_in, 16)
            load_ctx(0, 0, [NBLK - 1])
            load_ctx(0, 0, [1])
            load_turned(0, 0)
            load_ctx(0, 0, [2])
            sp.dma_start(res[:, D:].rearrange("p (t d) -> p t d", d=D),
                         x[P:, :].rearrange("(t p) d -> p t d", p=P)).then_inc(x_rest_in, 16)
            load_mask(0)
            load_ctx(1, 1, [NBLK - 1])
            load_ctx(1, 1, [1])
            load_turned(1, 0)
            load_ctx(1, 1, [2])
            sp.dma_start(gam, gamma.partition_broadcast(P)).then_inc(gb_in, 16)
            sp.dma_start(bet, beta.partition_broadcast(P)).then_inc(gb_in, 16)
            load_ctx(0, 0, [0])
            sp.wait_ge(bound_ready, 1)
            load_mask(1)
            load_ctx(1, 1, [0])
            with sp.Fori(1, TILES // 2) as h:
                for par in range(2):
                    p = h * 2 + par
                    load_turned(p, 0)
                    load_ctx(p, par)
            sp.wait_ge(pv_block, NBLK * (TILES - 1))
            sp.dma_start(wqkv_sb, w_qkv.rearrange("p (j k h) -> p j k h", j=3, k=KC)).then_inc(w_in, 16)
            sp.dma_start(wo_sb, w_out.rearrange("p (k h) -> p k h", k=KC)).then_inc(w_in, 16)
            sp.dma_start(rw_sb, w_router.rearrange("p (k e) -> p k e", k=KC)).then_inc(w_in, 16)
            sp.wait_ge(zero_set, 2)
            sp.dma_start(slots_m.rearrange("(s p) d -> p s d", p=P), nobody[:]).then_inc(zero_out, 16)
            sp.dma_start(tokens_x[TOKENS:TOKENS + P, :], zeros[:]).then_inc(zero_out, 16)
            sp.dma_start(acc[TOKENS:TOKENS + P, :], zeros[:]).then_inc(acc_set, 16)
            sp.wait_ge(pv_block, NBLK * TILES)
            for b in range(WB):
                load_block(sp, 0, b)
            with sp.Fori(0, TILES // 2) as h:
                for par in range(2):
                    t = h * 2 + par
                    sp.wait_ge(res2, t + 1)
                    sp.dma_start(acc[bass.ds(t * P, P), :], tile_of(t)).then_inc(acc_set, 16)
                    sp.wait_ge(xn2_ready, t + 1)
                    sp.dma_start(tokens_x[bass.ds(t * P, P), :], xr[par]).then_inc(x_out[par], 16)
            sp.wait_ge(acc_set, 16 * (TILES + 1))
            sp.wait_ge(added[0], 16 * ((SLOTS + 1) // 2))
            sp.wait_ge(added[1], 16 * (SLOTS // 2))

        @block.gpsimd
        def _(pool):
            own = Steps(pool, p_own)

            def bounds(p):
                pool.wait_ge(mask_in, p * 16 + 16)
                if not (isinstance(p, int) and p == 0):
                    pool.wait_ge(masked, p * 2)
                carry_pool_waits(pool, own)
                pool.tensor_scalar(bound, mask_sb, 0, MASKED - LIMIT, ALU.is_equal, ALU.mult).then_inc(bound_ready, 1)

            def residual(j):
                pool.wait_ge(att_ready, j + 1)
                own.then_next(pool.tensor_tensor(att, att, gam, ALU.mult))
                own.then_next(pool.tensor_tensor(att, att, bet, ALU.add))
                pool.tensor_tensor(tile_of(j), tile_of(j), att, ALU.add).then_inc(res1, 1)

            own.then_next(pool.memset(small[:, 21:22], 0.0))
            bounds(0)
            bounds(1)
            pool.wait_ge(gb_in, 32)
            with pool.Fori(0, TILES - 2) as j:
                own.enter(j, 3)
                bounds(j + 2)
                residual(j)
                own.leave(TILES - 2)
            residual(TILES - 2)
            residual(TILES - 1)

            def send(t, par):
                pool.wait_ge(pos_ready, t + 1)
                pool.wait_ge(places_free, t + TOP_K)
                carry_pool_waits(pool, own)
                for n in range(TOP_K):
                    where = bass.IndirectOffsetOnAxis(ap=pos[par][:, n:n + 1], axis=0)
                    pool.indirect_dma_start(out=slots_m, out_offset=where, in_=meta[par][:, n, :], in_offset=None
                                            ).then_inc(sent, 16)
                pool.wait_ge(sent, t * (16 * TOP_K) + 16 * TOP_K)
                pool.tensor_tensor(small[:, 23:24], small[:, 21:22], small[:, 21:22], ALU.add).then_inc(places_free, 1)

            for n in range(2):
                pool.memset(small[:, 24 + n:25 + n], 0.0).then_inc(places_free, 1)
            pool.wait_ge(zero_out, 32)
            with pool.Fori(0, TILES // 2) as h:
                own.enter(h, 2)
                for par in range(2):
                    send(h * 2 + par, par)
                own.leave(TILES // 2)

            def fetch(i, h, par):
                row = 0 if isinstance(i, int) and i == 0 else pool.value_load(
                    slot_at[0:1, bass.ds(i, 1)], min_val=0, max_val=(PLACES - 1) * P)
                if not (isinstance(i, int) and i < 2):
                    pool.wait_ge(added[par], h * 16)
                    pool.wait_ge(x_turned, i - 1)
                pool.dma_start(gm[par], slots_m[bass.ds(row, P), :]).then_inc(m_here[par], 16)
                pool.wait_ge(m_here[par], h * 16 + 16)
                carry_pool_waits(pool, own)
                pool.indirect_dma_start(
                    out=xg[par], out_offset=None, in_=tokens_x,
                    in_offset=bass.IndirectOffsetOnAxis(ap=gm[par].bitcast(I32)[:, 1:2], axis=0)
                ).then_inc(x_here[par], 16)

            def add(i, h, par):
                pool.wait_ge(y_ready, i + 1)
                if par:
                    pool.wait_ge(added[0], h * 16 + 16)
                elif not (isinstance(i, int) and i == 0):
                    pool.wait_ge(added[1], h * 16)
                carry_pool_waits(pool, own)
                pool.indirect_dma_start(
                    out=acc, out_offset=bass.IndirectOffsetOnAxis(ap=gm[par].bitcast(I32)[:, 1:2], axis=0),
                    in_=yb[par], in_offset=None, compute_op=ALU.add).then_inc(added[par], 16)

            for par in range(2):
                pool.wait_ge(x_out[par], 16 * (TILES // 2))
            fetch(0, 0, 0)
            pool.wait_ge(slot_ready, 1)
            fetch(1, 0, 1)
            pool.wait_ge(acc_set, 16 * (TILES + 1))
            with pool.Fori(0, SLOTS // 2 - 1) as h:
                own.enter(h, 4)
                for par in range(2):
                    add_first = h * 2 + par
                    add(add_first, h, par)
                    fetch(add_first + 2, h + 1, par)
                own.leave(SLOTS // 2 - 1)
            for i in range(SLOTS - 3, SLOTS):
                add(i, i // 2, i % 2)
                if i + 2 < SLOTS:
                    fetch(i + 2, i // 2 + 1, i % 2)

        @block.tensor
        def _(pe):
            tp = [bank(NBLK + n) for n in range(BANKS)]
            att_ps = bank(7)

            def open_fill(j, r):
                if (prev := bank_before(j, r)) is not None:
                    act, n = copied_at(*prev)
                    pe.wait_ge(copied[act], n)
                return tp[r % BANKS]

            def scores(p, par, j, blk):
                n = min(BLK, T - blk * BLK)
                if blk < LOADED_TURNED:
                    pe.wait_ge(ctxT_here[blk], p * 32 + 32)
                else:
                    last = FIRST_FILL[blk] + FILLS_BLK[blk] - 1
                    for by in (True, False):
                        r = max(r for r in range(last - BANKS + 1, last + 1) if by_act(r) == by)
                        act, count = copied_at(j, r)
                        pe.wait_ge(copied[act], count)
                if blk == 0 and not (isinstance(p, int) and p == 0):
                    pe.wait_ge(masked, p * 2)
                for k in range(KC):
                    for b in range(2):
                        mm = pe.matmul(ps[64 * b:64 * b + 64, blk * BLK:blk * BLK + n],
                                       xqT[par][:, k, 64 * b:64 * b + 64],
                                       ctxT[blk % 2][:, b, k, :] if blk < NBLK - 1 else ctxT_rest[:, b, k, :],
                                       start=(k == 0), stop=(k == KC - 1))
                mm.then_inc(scored, 1)

            def qk(p, h, par, j):
                pe.wait_ge(xq_ready, p + 1)
                o = open_fill(j, 0)
                for k in range(KC):
                    mm = pe.transpose(o[:, k * P:(k + 1) * P], xq[:, k * P:(k + 1) * P], ident)
                mm.then_inc(filled, 1)
                turn_ctx(h, par, j, NBLK - 1)
                turn_ctx(h, par, j, 1)
                for blk in range(NBLK):
                    if blk == 0:
                        act, count = copied_at(j, 0)
                        pe.wait_ge(copied[act], count)
                    scores(p, par, j, blk)
                    if blk == 0:
                        turn_ctx(h, par, j, 2)

            def turn_ctx(h, par, j, blk):
                pe.wait_ge(ctx_here[par][blk], h * 32 + 32)
                r = FIRST_FILL[blk]
                for b in range(2):
                    for k in range(KC):
                        if blk < NBLK - 1 or k == 0:
                            o = open_fill(j, r)
                        if blk < NBLK - 1:
                            for c in range(4):
                                mm = pe.transpose(o[:, c * P:(c + 1) * P],
                                                  ctxb[par][:, b, 4 * blk + c, k * P:(k + 1) * P], ident)
                        else:
                            mm = pe.transpose(o[:, k * P:k * P + T_REST],
                                              ctxb[par][0:T_REST, b, CHUNKS - 1, k * P:(k + 1) * P],
                                              ident[0:T_REST, 0:T_REST])
                        if blk < NBLK - 1 or k == KC - 1:
                            mm.then_inc(filled, 1)
                            r += 1

            def pv(j, h, par):
                pe.wait_ge(exp_done, j + 1)
                for n, blk in enumerate(SUM_ORDER):
                    o = open_fill(j, QK_FILLS + n)
                    for c in range(4 * blk, min(4 * blk + 4, CHUNKS)):
                        m = P if c < CHUNKS - 1 else T_REST
                        mm = pe.transpose(o[0:m, (c % 4) * P:(c % 4 + 1) * P], prob[:, c * P:c * P + m], ident)
                    mm.then_inc(filled, 1)
                if not (isinstance(j, int) and j == 0):
                    pe.wait_ge(att_read, j)
                for n, blk in enumerate(SUM_ORDER):
                    act, count = copied_at(j, QK_FILLS + n)
                    pe.wait_ge(copied[act], count)
                    if blk < LOADED_TURNED:
                        pe.wait_ge(ctx_here[par][blk], h * 32 + 32)
                    chunks = range(4 * blk, min(4 * blk + 4, CHUNKS))
                    for c in chunks:
                        m = P if c < CHUNKS - 1 else T_REST
                        for b in range(2):
                            mm = pe.matmul(att_ps[64 * b:64 * b + 64, :], probT[0:m, c, 64 * b:64 * b + 64],
                                           ctxb[par][0:m, b, c, :], start=(n == 0 and c == chunks[0]),
                                           stop=(n == NBLK - 1 and c == chunks[-1]))
                    mm.then_inc(pv_block, 1)

            pe.wait_ge(cst_in, 16)
            qk(0, 0, 0, -1)
            qk(1, 0, 1, 0)
            pv(0, 0, 0)
            with pe.Fori(0, TILES // 2 - 1) as h:
                for par in range(2):
                    j = h * 2 + (1 + par)
                    qk(j + 1, h + 1, par, j)
                    pv(j, h + par, 1 - par)
            pv(TILES - 1, TILES // 2 - 1, 1)

            S, TB, QB, KB, VB, MB, CB, OB = (bank(n) for n in range(8))

            def turn_first(j, par):
                pe.wait_ge(xn_ready, j + 1)
                for k in range(KC):
                    mm = pe.transpose(TB[:, k * P:(k + 1) * P], xn[par][:, k * P:(k + 1) * P], ident)
                mm.then_inc(t1_done, 1)

            def project(j, par, which, dst, copied_out, done, hcs=range(KC)):
                if 0 in hcs:
                    pe.wait_ge(t1_copied, j + 1)
                    if not isinstance(j, int) or j >= 1:
                        pe.wait_ge(copied_out, j)
                for hc in hcs:
                    for k in range(KC):
                        mm = pe.matmul(dst[:, hc * P:(hc + 1) * P], wqkv_sb[:, which, k, hc * P:(hc + 1) * P],
                                       xnT[par][:, k, :], start=(k == 0), stop=(k == KC - 1))
                if KC - 1 in hcs:
                    mm.then_inc(done, 1)

            def values(j, par):
                if not isinstance(j, int) or j >= 1:
                    pe.wait_ge(v_copied, j)
                for k in range(KC):
                    mm = pe.matmul(VB, xnT[par][:, k, :], wqkv_sb[:, 2, k, :], start=(k == 0), stop=(k == KC - 1))
                mm.then_inc(v_done, 1)

            def own_scores(j, par):
                pe.wait_ge(q_copied, j + 1)
                pe.wait_ge(k_copied, j + 1)
                if not isinstance(j, int) or j >= 1:
                    pe.wait_ge(e_done, j)
                if not isinstance(j, int) or j >= 3:
                    pe.wait_ge(picked, j - 1)
                for k in range(KC):
                    mm = pe.matmul(S[:, 0:P], qT[par][:, k, :], kT[par][:, k, :], start=(k == 0), stop=(k == KC - 1))
                mm.then_inc(s_done, 1)

            def turn_probs(j, par):
                pe.wait_ge(pr_ready, j + 1)
                pe.transpose(MB[:, 0:P], pr[par], ident).then_inc(pt_done, 1)

            def weigh(j, par):
                pe.wait_ge(pt_copied, j + 1)
                pe.wait_ge(v_copied, j + 1)
                if not isinstance(j, int) or j >= 1:
                    pe.wait_ge(ct_copied, j)
                for hc in range(KC):
                    mm = pe.matmul(CB[:, hc * P:(hc + 1) * P], vv[par][:, hc * P:(hc + 1) * P], prT,
                                   start=True, stop=True)
                mm.then_inc(ct_done, 1)

            def project_out(j):
                pe.wait_ge(ct_copied, j + 1)
                if not isinstance(j, int) or j >= 1:
                    pe.wait_ge(res2, j)
                for hc in range(KC):
                    mm = pe.matmul(OB, cT[:, hc, :], wo_sb[:, hc, :], start=(hc == 0), stop=(hc == KC - 1))
                mm.then_inc(o_done, 1)

            def turn_second(j, par, first):
                pe.wait_ge(xn2_ready, j + 1)
                pe.wait_ge(t1_copied, first)
                for k in range(KC):
                    mm = pe.transpose(TB[:, k * P:(k + 1) * P], xr[par][:, k * P:(k + 1) * P], ident)
                mm.then_inc(t2_done, 1)

            def router(j):
                pe.wait_ge(t2_copied, j + 1)
                for k in range(KC):
                    mm = pe.matmul(MB[:, P:P + EXPERTS], xrT[:, k, :], rw_sb[:, k, :],
                                   start=(k == 0), stop=(k == KC - 1))
                mm.then_inc(r_done, 1)

            def ranks(j, par):
                pe.wait_ge(picked, j + 1)
                pe.matmul(S[:, P:P + EXPERTS], before_me, both[par], start=True, stop=False)
                pe.matmul(S[:, P:P + EXPERTS], ones, cum[par], start=False, stop=True).then_inc(rank_done, 1)

            def tile_step(j, par, front, back, back2):
                if front:
                    turn_first(j + 1, 1 - par)
                own_scores(j, par)
                if front:
                    project(j + 1, 1 - par, 0, QB, q_copied, q_done)
                    project(j + 1, 1 - par, 1, KB, k_copied, k_done, range(2))
                if back:
                    turn_second(j - 1, 1 - par, j + 2 if front else TILES)
                turn_probs(j, par)
                if front:
                    project(j + 1, 1 - par, 1, KB, k_copied, k_done, range(2, KC))
                weigh(j, par)
                if back2:
                    ranks(j - 2, par)
                if back:
                    router(j - 1)
                if front:
                    values(j + 1, 1 - par)
                project_out(j)

            pe.wait_ge(w_in, 48)
            turn_first(0, 0)
            project(0, 0, 0, QB, q_copied, q_done)
            project(0, 0, 1, KB, k_copied, k_done)
            values(0, 0)
            pe.wait_ge(att_read, TILES)
            tile_step(0, 0, True, False, False)
            tile_step(1, 1, True, True, False)
            with pe.Fori(1, TILES // 2 - 1) as h:
                for par in range(2):
                    tile_step(h * 2 + par, par, True, True, True)
            tile_step(TILES - 2, 0, True, True, True)
            tile_step(TILES - 1, 1, False, True, True)
            turn_second(TILES - 1, 1, TILES)
            router(TILES - 1)
            pe.wait_ge(pos_ready, TILES - 2)
            ranks(TILES - 2, 0)
            pe.wait_ge(pos_ready, TILES - 1)
            ranks(TILES - 1, 1)
            pe.matmul(bank(6)[:, 0:EXPERTS], ones, cum[TILES % 2], start=True, stop=True).then_inc(count_done, 1)

            UB, HB, YB, XB = [bank(0), bank(1), bank(2)], [bank(3), bank(4)], [bank(5), bank(6)], bank(7)

            def turn_x(i, h, par):
                pe.wait_ge(x_here[par], h * 16 + 16)
                if not isinstance(i, int) or i >= 1:
                    pe.wait_ge(x_ready, i)
                for k in range(KC):
                    mm = pe.transpose(XB[:, k * P:(k + 1) * P], xg[par][:, k * P:(k + 1) * P], ident)
                mm.then_inc(x_turned, 1)

            def product(out, rows, b, k, start, stop):
                high, low = w_high[b][:, k * BLK:(k + 1) * BLK], w_low[:, b, k * BLK:(k + 1) * BLK]
                pe.matmul(out, rows[0], high, start=start, stop=False)
                pe.matmul(out, rows[0], low, start=False, stop=False)
                return pe.matmul(out, rows[1], high, start=False, stop=stop)

            def up(i, e, par, f):
                pe.wait_ge(w_ready, e * WB + (f + 1))
                if not (isinstance(i, int) and i == 0 and f < 3):
                    pe.wait_ge(gelu_done, i * FB + (f - 2))
                for k in range(KC):
                    mm = product(UB[f % 3], [part[:, k, :] for part in xT_parts[par]], f, k, k == 0, k == KC - 1)
                mm.then_inc(up_done, 1)

            def turn_h(i, f):
                pe.wait_ge(gelu_done, i * FB + (f + 1))
                if not (isinstance(i, int) and i == 0 and f < 2):
                    pe.wait_ge(h_ready, i * FB + (f - 1))
                for c in range(4):
                    mm = pe.transpose(HB[f % 2][:, c * P:(c + 1) * P], hid[:, f * BLK + c * P:f * BLK + (c + 1) * P], ident)
                mm.then_inc(h_turned, 1)

            def down(i, e, par, f):
                pe.wait_ge(h_ready, i * FB + (f + 1))
                pe.wait_ge(w_ready, e * WB + (FB + f + 1))
                for c in range(4):
                    mm = product(YB[par], [h_parts[:, part, 4 * f + c, :] for part in range(2)], FB + f, c,
                                 f == 0 and c == 0, f == FB - 1 and c == 3)
                mm.then_inc(down_done, 1)

            def slot(i, h, par, last=False):
                e = 0 if isinstance(i, int) and i == 0 else pe.value_load(
                    slot_e[0:1, bass.ds(i, 1)], min_val=0, max_val=EXPERTS - 1)
                pe.wait_ge(x_ready, i + 1)
                up(i, e, par, 0)
                up(i, e, par, 1)
                turn_h(i, 0)
                up(i, e, par, 2)
                turn_h(i, 1)
                up(i, e, par, 3)
                turn_h(i, 2)
                if not isinstance(i, int) or i >= 2:
                    pe.wait_ge(y_ready, i - 1)
                down(i, e, par, 0)
                down(i, e, par, 1)
                turn_h(i, 3)
                if not last:
                    turn_x(i + 1, h + par, 1 - par)
                down(i, e, par, 2)
                down(i, e, par, 3)

            turn_x(0, 0, 0)
            slot(0, 0, 0)
            pe.wait_ge(slot_ready, 1)
            slot(1, 0, 1)
            with pe.Fori(1, SLOTS // 2) as h:
                for par in range(2):
                    slot(h * 2 + par, h, par)
            slot(SLOTS - 1, SLOTS // 2, 0, last=True)

        @block.scalar
        def _(act):
            def copy_out(j, p, par, r):
                act.wait_ge(filled, filled_at(j, r))
                place(act, j, p, par, r).then_inc(copied[True], 1)

            def qk_copies(j, p, par):
                for r in range(QK_FILLS):
                    if by_act(r):
                        copy_out(j, p, par, r)

            def exps(j, par):
                act.wait_ge(negtop_ready, j + 1)
                nc.scalar.activation(prob, prob, ACT.Exp, bias=negtop[:, par:par + 1], scale=1.0,
                                     accum_out=rowsum[:, par:par + 1]).then_inc(exp_done, 1)

            def p_copies(j):
                for r in range(QK_FILLS, FILLS):
                    if by_act(r):
                        copy_out(j, j, 0, r)

            act.wait_ge(cst_in, 16)
            qk_copies(-1, 0, 0)
            exps(0, 0)
            qk_copies(0, 1, 1)
            p_copies(0)
            with act.Fori(0, TILES // 2 - 1) as h:
                for par in range(2):
                    j = h * 2 + (1 + par)
                    exps(j, 1 - par)
                    qk_copies(j, j + 1, par)
                    p_copies(j)
            exps(TILES - 1, 1)
            p_copies(TILES - 1)

            def copy_t1(j, par):
                act.wait_ge(t1_done, j + 1)
                if not isinstance(j, int) or j >= 2:
                    act.wait_ge(v_done, j - 1)
                act.copy(xnT[par], bank(1).rearrange("p (k t) -> p k t", k=KC)).then_inc(t1_copied, 1)

            def copy_qkv(j, par):
                for n, (done, copied_out, dst) in enumerate(((q_done, q_copied, qT), (k_done, k_copied, kT),
                                                             (v_done, v_copied, vv))):
                    act.wait_ge(done, j + 1)
                    if not isinstance(j, int) or j >= 2:
                        act.wait_ge(s_done if n < 2 else ct_done, j - 1)
                    src = bank(2 + n)
                    if n < 2:
                        src = src.rearrange("p (k t) -> p k t", k=KC)
                    act.copy(dst[par], src).then_inc(copied_out, 1)

            def own_exps(j, par):
                act.wait_ge(top_ready, j + 1)
                for b in range(2):
                    q = slice(64 * b, 64 * b + 64)
                    e = nc.scalar.activation(pr[par][q, 64 * b:64 * b + 64], bank(0)[q, 64 * b:64 * b + 64], ACT.Exp,
                                             bias=negtop[q, par:par + 1], scale=SCALE,
                                             accum_out=rowsum[q, par:par + 1])
                e.then_inc(e_done, 1)

            def gate_exp(j, par):
                act.wait_ge(picked, j + 1)
                nc.scalar.activation(ratio[par], ratio[par], ACT.Exp).then_inc(ratio_ready, 1)

            copy_t1(0, 0)
            copy_qkv(0, 0)
            act.wait_ge(pr_clear, 2)
            copy_t1(1, 1)
            own_exps(0, 0)
            copy_qkv(1, 1)
            copy_t1(2, 0)
            own_exps(1, 1)
            copy_qkv(2, 0)
            with act.Fori(1, TILES // 2 - 1) as h:
                for par in range(2):
                    j = h * 2 + par
                    copy_t1(j + 1, 1 - par)
                    own_exps(j, par)
                    gate_exp(j - 2, par)
                    copy_qkv(j + 1, 1 - par)
            for j in range(TILES - 2, TILES):
                if j + 1 < TILES:
                    copy_t1(j + 1, 1 - j % 2)
                own_exps(j, j % 2)
                gate_exp(j - 2, j % 2)
                if j + 1 < TILES:
                    copy_qkv(j + 1, 1 - j % 2)

            def split_high(e, b):
                act.wait_ge(raw_here[b], e * 16 + 16)
                act.copy(w_high[b], w_raw[b]).then_inc(w_high_ready, 1)

            def expert(i):
                return act.value_load(slot_e[0:1, bass.ds(i, 1)], min_val=0, max_val=EXPERTS - 1)

            def gelu(i, f):
                act.wait_ge(up_done, i * FB + (f + 1))
                if not (isinstance(i, int) and i == 0):
                    act.wait_ge(h_turned, i * FB + (f - FB + 1))
                nc.scalar.activation(hid[:, f * BLK:(f + 1) * BLK], bank(f % 3), ACT.Gelu).then_inc(gelu_done, 1)

            def high_h(i, f):
                act.wait_ge(h_turned, i * FB + (f + 1))
                if not (isinstance(i, int) and i == 0):
                    act.wait_ge(down_done, i * FB + (f - FB + 1))
                act.copy(h_parts[:, 0, 4 * f:4 * f + 4, :], bank(3 + f % 2).rearrange("p (c t) -> p c t", c=4)
                         ).then_inc(h_high_ready, 1)

            def high_x(i, par):
                act.wait_ge(x_turned, i + 1)
                act.copy(xT_parts[par][0], bank(7).rearrange("p (k t) -> p k t", k=KC)).then_inc(x_high_ready, 1)

            def slot(i, par, last=False):
                static = isinstance(i, int)
                e = 0 if static and i == 0 else expert(i)
                first = None if static and i == 0 else (e > expert(i - 1))
                after = None if last else expert(i + 1)

                def if_first(b):
                    if first is None:
                        split_high(e, b)
                    else:
                        with act.If(first):
                            split_high(e, b)

                gelu(i, 0)
                if_first(6)
                gelu(i, 1)
                if not last:
                    with act.If(after > e):
                        load_block(act, after, 0)
                        load_block(act, after, 1)
                high_h(i, 0)
                if_first(7)
                gelu(i, 2)
                high_h(i, 1)
                if not last:
                    with act.If(after > e):
                        load_block(act, after, 2)
                        split_high(after, 0)
                gelu(i, 3)
                high_h(i, 2)
                if not last:
                    with act.If(after > e):
                        load_block(act, after, 3)
                        split_high(after, 1)
                        act.wait_ge(down_done, i * FB + 1)
                        load_block(act, after, 4)
                        split_high(after, 2)
                high_h(i, 3)
                if not last:
                    high_x(i + 1, 1 - par)
                    with act.If(after > e):
                        for b in range(5, WB):
                            act.wait_ge(down_done, i * FB + (b - FB + 1))
                            load_block(act, after, b)
                            split_high(after, b - 2)

            for b in range(2):
                split_high(0, b)
            gate_exp(TILES - 2, 0)
            gate_exp(TILES - 1, 1)
            act.wait_ge(res1, TILES)
            for b in range(2, 5):
                split_high(0, b)
            act.wait_ge(o_done, TILES)
            split_high(0, 5)
            high_x(0, 0)
            act.wait_ge(slot_ready, 1)
            slot(0, 0)
            slot(1, 1)
            with act.Fori(1, SLOTS // 2) as h:
                for par in range(2):
                    slot(h * 2 + par, par)
            slot(SLOTS - 1, 0, last=True)

        @block.vector
        def _(dve):
            own = Steps(dve, v_own)

            def rsqrt_start(v, variance):
                own.then_next(dve.tensor_scalar(v, variance, EPS, None, ALU.add))
                own.then_next(dve.tensor_scalar(rstd.bitcast(I32), v.bitcast(I32), -0.5, GUESS, ALU.mult, ALU.add))

            def rsqrt_step(v):
                own.then_next(dve.scalar_tensor_tensor(out=half, in0=rstd, scalar=rstd, in1=v,
                                                       op0=ALU.mult, op1=ALU.mult))
                own.then_next(dve.tensor_scalar(half, half, -0.5, 1.5, ALU.mult, ALU.add))
                own.then_next(dve.tensor_tensor(rstd, rstd, half, ALU.mult))

            def moments(src):
                carry_waits(dve)
                own.then_next(dve.bn_stats(stats, src))
                carry_waits(dve)
                own.then_next(dve.bn_aggr(mv, stats))

            NORM = 2 + 2 + 3 * NEWTON

            def normalize(dst, src):
                moments(src)
                rsqrt_start(var, mv[:, 1:2])
                for _ in range(NEWTON):
                    rsqrt_step(var)
                return dve.tensor_scalar(dst, src, mv[:, 0:1], rstd, ALU.subtract, ALU.mult)

            def queries(p):
                if not isinstance(p, int) or p >= 1:
                    dve.wait_ge(filled, filled_at(p - 2 if not isinstance(p, int) or p > 1 else -1, 0))
                normalize(xq, tile_of(p)).then_inc(xq_ready, 1)

            def softmax(j, par):
                dve.wait_ge(bound_ready, j + 1)
                if not isinstance(j, int) or j >= 1:
                    dve.wait_ge(filled, filled_at(j - 1, FILLS - 1))
                for n, (a, b) in enumerate(((0, 2 * BLK), (2 * BLK, T))):
                    dve.wait_ge(scored, j * NBLK + (2 * n + 2))
                    dve.scalar_tensor_tensor(out=prob[:, a:b], in0=bound[:, a:b], scalar=LIMIT, in1=ps[:, a:b],
                                             op0=ALU.add, op1=ALU.min).then_inc(masked, 1)
                dve.wait_ge(masked, j * 2 + 2)
                own.then_next(dve.tensor_reduce(top, prob, AX.X, ALU.max))
                dve.tensor_scalar(negtop[:, par:par + 1], top, -1.0, None, ALU.mult).then_inc(negtop_ready, 1)

            def attended(j, par):
                dve.wait_ge(pv_block, j * NBLK + NBLK)
                own.then_next(dve.reciprocal(inv, rowsum[:, par:par + 1]))
                if not isinstance(j, int) or j >= 1:
                    dve.wait_ge(res1, j)
                dve.tensor_scalar(att, bank(7), inv, None, ALU.mult).then_inc(att_read, 1)
                dve.wait_ge(att_read, j + 1)

            def attended_norm(part):
                if part == 0:
                    moments(att)
                if part == 1:
                    rsqrt_start(var, mv[:, 1:2])
                if 2 <= part < 2 + NEWTON:
                    rsqrt_step(var)
                if part == 2 + NEWTON:
                    dve.tensor_scalar(att, att, mv[:, 0:1], rstd, ALU.subtract, ALU.mult).then_inc(att_ready, 1)

            def copies(j, p, par, rs):
                for r in rs:
                    if not by_act(r):
                        dve.wait_ge(filled, filled_at(j, r))
                        place(dve, j, p, par, r).then_inc(copied[False], 1)

            dve.wait_ge(x_in, 16)
            queries(0)
            dve.memset(zeros[:], 0.0).then_inc(zero_set, 1)
            own.then_next(dve.memset(nobody[:, :, 0], 0.0))
            dve.wait_ge(cst_in, 16)
            dve.tensor_scalar(nobody[:, :, 1].bitcast(I32), nobody[:, :, 0], spare, None, ALU.add
                              ).then_inc(zero_set, 1)
            copies(-1, 0, 0, range(QK_FILLS))
            dve.wait_ge(x_rest_in, 16)
            queries(1)
            softmax(0, 0)
            copies(0, 1, 1, range(FILLS))
            with dve.Fori(0, TILES // 2 - 1) as h:
                own.enter(h, 2 * (NORM + 1 + 1 + NORM))
                for par in range(2):
                    j = h * 2 + (1 + par)
                    queries(j + 1)
                    softmax(j, 1 - par)
                    copies(j, j + 1, par, range(4))
                    attended(j - 1, par)
                    for part in range(3 + NEWTON):
                        copies(j, j + 1, par, range(4 + 3 * part, min(7 + 3 * part, FILLS)))
                        attended_norm(part)
                    copies(j, j + 1, par, range(4 + 3 * (3 + NEWTON), FILLS))
                own.leave(TILES // 2 - 1)
            softmax(TILES - 1, 1)
            copies(TILES - 1, TILES - 1, 1, range(QK_FILLS, FILLS))
            attended(TILES - 2, 0)
            for part in range(3 + NEWTON):
                attended_norm(part)
            for i in range(2):
                dve.memset(pr[i], 0.0).then_inc(pr_clear, 1)

            def first_norm(j, par):
                dve.wait_ge(res1, j + 1)
                if not isinstance(j, int) or j >= 2:
                    dve.wait_ge(t1_done, j - 1)
                normalize(xn[par], tile_of(j)).then_inc(xn_ready, 1)

            def tops(j, par):
                dve.wait_ge(s_done, j + 1)
                for b in range(2):
                    q = slice(64 * b, 64 * b + 64)
                    own.then_next(dve.tensor_reduce(top[q, :], bank(0)[q, 64 * b:64 * b + 64], AX.X, ALU.max))
                dve.tensor_scalar(negtop[:, par:par + 1], top, -SCALE, None, ALU.mult).then_inc(top_ready, 1)

            def probs(j, par):
                dve.wait_ge(e_done, j + 1)
                own.then_next(dve.reciprocal(inv, rowsum[:, par:par + 1]))
                dve.tensor_scalar(pr[par], pr[par], inv, None, ALU.mult).then_inc(pr_ready, 1)

            def copy_pt(j):
                dve.wait_ge(pt_done, j + 1)
                if not isinstance(j, int) or j >= 1:
                    dve.wait_ge(ct_done, j)
                dve.tensor_copy(prT, bank(5)[:, 0:P]).then_inc(pt_copied, 1)

            def copy_ct(j):
                dve.wait_ge(ct_done, j + 1)
                if not isinstance(j, int) or j >= 1:
                    dve.wait_ge(o_done, j)
                dve.tensor_copy(cT, bank(6).rearrange("p (k t) -> p k t", k=KC)).then_inc(ct_copied, 1)

            def copy_t2(j):
                dve.wait_ge(t2_done, j + 1)
                if not isinstance(j, int) or j >= 1:
                    dve.wait_ge(r_done, j)
                dve.tensor_copy(xrT, bank(1).rearrange("p (k t) -> p k t", k=KC)).then_inc(t2_copied, 1)

            def route_first(j, par):
                dve.wait_ge(r_done, j + 1)
                own.then_next(dve.tensor_copy(logit, bank(5)[:, P:P + EXPERTS]))
                src = logit
                for n in range(TOP_K):
                    own.then_next(dve.tensor_reduce(best[:, n:n + 1], src, AX.X, ALU.max))
                    own.then_next(dve.tensor_scalar(tmp, src, best[:, n:n + 1], -100.0, ALU.is_equal, ALU.mult))
                    own.then_next(dve.tensor_tensor(tmp, tmp, expert_no, ALU.add))
                    own.then_next(dve.tensor_reduce(low, tmp, AX.X, ALU.min))
                    own.then_next(dve.tensor_scalar(pick[par][n], tmp, low, None, ALU.is_equal))
                    if n == 0:
                        own.then_next(dve.scalar_tensor_tensor(out=logit2, in0=pick[par][0], scalar=-HUGE, in1=logit,
                                                               op0=ALU.mult, op1=ALU.add))
                        src = logit2
                own.then_next(dve.tensor_tensor(ratio[par], best[:, 1:2], best[:, 0:1], ALU.subtract))
                own.then_next(dve.tensor_tensor(both[par], pick[par][0], pick[par][1], ALU.add))
                dve.tensor_tensor(cum[1 - par], cum[par], both[par], ALU.add).then_inc(picked, 1)

            FIRST_STEPS = 1 + 5 * TOP_K + 1 + 2

            def route_second(j, par):
                dve.wait_ge(places_free, j + 1)
                dve.wait_ge(rank_done, j + 1)
                own.then_next(dve.tensor_tensor(rank, bank(0)[:, P:P + EXPERTS], room_at, ALU.add))
                for n in range(TOP_K):
                    own.then_next(dve.tensor_tensor(tmp, pick[par][n], rank, ALU.mult))
                    own.then_next(dve.tensor_reduce(posf, tmp, AX.X, ALU.add))
                    own.then_next(dve.tensor_copy(pos[par][:, n:n + 1], posf))
                    own.then_next(dve.tensor_copy(meta_i[par][:, n, 1:2], token))
                dve.wait_ge(ratio_ready, j + 1)
                own.then_next(dve.tensor_scalar(low, ratio[par], 1.0, None, ALU.add))
                own.then_next(dve.reciprocal(meta[par][:, 0, 0:1], low))
                own.then_next(dve.tensor_tensor(meta[par][:, 1, 0:1], ratio[par], meta[par][:, 0, 0:1], ALU.mult))
                dve.tensor_scalar(token, token, float(P), None, ALU.add).then_inc(pos_ready, 1)
                dve.wait_ge(pos_ready, j + 1)

            SECOND_STEPS = 1 + 4 * TOP_K + 3

            def second_norm(j, h, par):
                dve.wait_ge(o_done, j + 1)
                dve.tensor_tensor(tile_of(j), bank(7), tile_of(j), ALU.add).then_inc(res2, 1)
                dve.wait_ge(res2, j + 1)
                if not isinstance(j, int) or j >= 2:
                    dve.wait_ge(x_out[par], h * 16)
                normalize(xr[par], tile_of(j)).then_inc(xn2_ready, 1)

            def tile_step(j, h, par, front, back, back2):
                tops(j, par)
                probs(j, par)
                if back:
                    copy_t2(j - 1)
                copy_pt(j)
                if front:
                    first_norm(j + 2, par)
                copy_ct(j)
                if back2:
                    route_second(j - 2, par)
                if back:
                    route_first(j - 1, 1 - par)
                second_norm(j, h, par)

            own.then_next(dve.memset(cum[0], 0.0))
            own.then_next(dve.tensor_copy(token, me))
            first_norm(0, 0)
            first_norm(1, 1)
            attended(TILES - 1, 1)
            for part in range(3 + NEWTON):
                attended_norm(part)
            tile_step(0, 0, 0, True, False, False)
            tile_step(1, 0, 1, True, True, False)
            with dve.Fori(1, TILES // 2 - 1) as h:
                own.enter(h - 1, 2 * (2 + 1 + 2 * NORM + FIRST_STEPS + SECOND_STEPS))
                for par in range(2):
                    tile_step(h * 2 + par, h, par, True, True, True)
                own.leave(TILES // 2 - 2)
            for j in range(TILES - 2, TILES):
                tile_step(j, j // 2, j % 2, False, True, True)
            copy_t2(TILES - 1)
            route_second(TILES - 2, 0)
            route_first(TILES - 1, 1)

            def split_low(e, b):
                dve.wait_ge(w_high_ready, e * WB + (b + 1))
                dve.tensor_tensor(w_low[:, b, :], w_raw[b], w_high[b].bitcast(F32), ALU.subtract).then_inc(w_ready, 1)

            def low_x(i, par):
                dve.wait_ge(x_high_ready, i + 1)
                dve.tensor_tensor(xT_parts[par][1], bank(7).rearrange("p (k t) -> p k t", k=KC),
                                  xT_parts[par][0].bitcast(F32), ALU.subtract).then_inc(x_ready, 1)

            split_low(0, 0)
            route_second(TILES - 1, 1)
            split_low(0, 1)
            split_low(0, 2)
            low_x(0, 0)

            dve.wait_ge(count_done, 1)
            own.then_next(dve.tensor_scalar(cnt_i, bank(6)[:, 0:EXPERTS], float(P - 1), None, ALU.add))
            own.then_next(dve.tensor_scalar(cnt_r, cnt_i, 7, None, ALU.logical_shift_right))
            own.then_next(dve.tensor_scalar(lots, cnt_r, 1.0, None, ALU.max))
            own.then_next(dve.memset(ends[:, 0:1], 0.0))
            for e in range(EXPERTS):
                own.then_next(dve.tensor_tensor(ends[:, e + 1:e + 2], ends[:, e:e + 1], lots[:, e:e + 1], ALU.add))
            wide = [P, SLOTS, EXPERTS]
            own.then_next(dve.tensor_tensor(past, slot_no, ends[:, 1:].unsqueeze(1).to_broadcast(wide), ALU.is_ge))
            own.then_next(dve.tensor_reduce(before_f, past, AX.X, ALU.add))
            own.then_next(dve.tensor_tensor(weighed, past, lots.unsqueeze(1).to_broadcast(wide), ALU.mult))
            own.then_next(dve.tensor_reduce(taken, weighed, AX.X, ALU.add))
            own.then_next(dve.tensor_scalar(slot_e, before_f, float(EXPERTS - 1), None, ALU.min))
            own.then_next(dve.scalar_tensor_tensor(out=slot_f, in0=before_f, scalar=float(ROOM), in1=slot_no[:, :, 0],
                                                   op0=ALU.mult, op1=ALU.add))
            own.then_next(dve.tensor_tensor(slot_f, slot_f, taken, ALU.subtract))
            dve.tensor_scalar(slot_at, slot_f, float(PLACES - 1), float(P), ALU.min, ALU.mult).then_inc(slot_ready, 1)

            def low_h(i, f):
                dve.wait_ge(h_high_ready, i * FB + (f + 1))
                chunks = slice(4 * f, 4 * f + 4)
                dve.tensor_tensor(h_parts[:, 1, chunks, :], bank(3 + f % 2).rearrange("p (c t) -> p c t", c=4),
                                  h_parts[:, 0, chunks, :].bitcast(F32), ALU.subtract).then_inc(h_ready, 1)

            def copy_y(i, h, par):
                dve.wait_ge(down_done, i * FB + FB)
                if not isinstance(i, int) or i >= 2:
                    dve.wait_ge(added[par], h * 16)
                dve.wait_ge(m_here[par], h * 16 + 16)
                dve.tensor_scalar(yb[par], bank(5 + par), gm[par][:, 0:1], None, ALU.mult).then_inc(y_ready, 1)

            def expert(i):
                return dve.value_load(slot_e[0:1, bass.ds(i, 1)], min_val=0, max_val=EXPERTS - 1)

            def slot(i, h, par, last=False):
                static = isinstance(i, int)
                e = 0 if static and i == 0 else expert(i)
                first = None if static and i == 0 else (e > expert(i - 1))
                after = None if last else expert(i + 1)

                def if_first(*blocks):
                    if first is None:
                        for b in blocks:
                            split_low(e, b)
                    else:
                        with dve.If(first):
                            for b in blocks:
                                split_low(e, b)

                def if_after(*blocks):
                    if not last:
                        with dve.If(after > e):
                            for b in blocks:
                                split_low(after, b)

                if_first(5, 6)
                low_h(i, 0)
                if_first(7)
                low_h(i, 1)
                if_after(0)
                low_h(i, 2)
                if_after(1, 2)
                low_h(i, 3)
                if not last:
                    low_x(i + 1, 1 - par)
                if_after(3, 4)
                copy_y(i, h, par)

            dve.wait_ge(slot_ready, 1)
            split_low(0, 3)
            split_low(0, 4)
            slot(0, 0, 0)
            slot(1, 0, 1)
            with dve.Fori(1, SLOTS // 2) as h:
                for par in range(2):
                    slot(h * 2 + par, h, par)
            slot(SLOTS - 1, SLOTS // 2, 0, last=True)


def kernel(x, ctx_1024, mask_BxSxS2_ik1, L0_xattn_gamma, L0_xattn_beta, L0_attn_W_qkv, L0_attn_W_out,
           L0_ffn_router_w, L0_ffn_expert_w1, L0_ffn_expert_w2):
    import numpy as np
    import concourse.bacc as bacc
    from concourse.bass_utils import run_bass_kernel_spmd

    c = np.zeros((P, C_END), np.float32)
    c[:, C_ID:C_ID + P] = np.eye(P)
    c[:, C_TRI:C_TRI + P] = np.triu(np.ones((P, P)), 1)
    c[:, C_ONE:C_ONE + P] = 1.0
    c[:, C_ME] = np.arange(P)
    c[:, C_SPARE] = TOKENS + np.arange(P)
    c[:, C_EXP:C_ROOM] = np.arange(EXPERTS)
    c[:, C_ROOM:C_SLOT] = np.arange(EXPERTS) * TOKENS
    c[:, C_SLOT:C_END] = np.repeat(np.arange(SLOTS), EXPERTS)
    a = {
        "x": np.asarray(x).reshape(TILES * P, D),
        "ctx": np.asarray(ctx_1024),
        "ctx_turned": np.asarray(ctx_1024)[:, :LOADED_TURNED * BLK, :].reshape(BATCH, LOADED_TURNED, BLK, KC, P)
        .transpose(0, 4, 1, 3, 2)[:, :, ::-1],
        "mask": np.asarray(mask_BxSxS2_ik1).reshape(TILES * P, T),
        "gamma": np.asarray(L0_xattn_gamma),
        "beta": np.asarray(L0_xattn_beta),
        "w_qkv": np.asarray(L0_attn_W_qkv).reshape(D, 3, KC, P).transpose(3, 1, 2, 0).reshape(P, -1),
        "w_out": np.asarray(L0_attn_W_out).reshape(D, KC, P).transpose(2, 1, 0).reshape(P, -1),
        "w_router": np.asarray(L0_ffn_router_w).reshape(EXPERTS, KC, P).transpose(2, 1, 0).reshape(P, -1),
        "w1": np.asarray(L0_ffn_expert_w1).reshape(EXPERTS, FB, BLK, KC, P).transpose(0, 4, 1, 3, 2)
        .reshape(EXPERTS, P, -1),
        "w2": np.asarray(L0_ffn_expert_w2).reshape(EXPERTS, D, FC, P).transpose(0, 3, 2, 1).reshape(EXPERTS, P, -1),
        "consts": c,
    }
    a = {f"in_{k}": np.ascontiguousarray(v) for k, v in a.items()}
    nc = bacc.Bacc("TRN2", target_bir_lowering=False, num_devices=1)
    args = [nc.dram_tensor(k, v.shape, mybir.dt.from_np(v.dtype), kind="ExternalInput").ap() for k, v in a.items()]
    out = nc.dram_tensor("out_0", (TOKENS + P, D), F32, kind="ExternalOutput").ap()
    build(nc, *args, out)
    r = run_bass_kernel_spmd(nc, [a], core_ids=[0])
    return np.asarray(r.results[0]["out_0"])[:TOKENS].reshape(BATCH, SEQ, D)
```

```python
from contextlib import ExitStack

import concourse.bass as bass
from concourse import mybir

ALU = mybir.AluOpType
ACT = mybir.ActivationFunctionType
AX = mybir.AxisListType
F32 = mybir.dt.float32
F32R = mybir.dt.float32r
I32 = mybir.dt.int32

P = 128
BATCH, SEQ, D = 16, 64, 512
T = 1601
TILES = BATCH * SEQ // P
KC = D // P
BLK = 512
CHUNKS = -(-T // P)
T_REST = T - (CHUNKS - 1) * P
NBLK = -(-T // BLK)
EXPERTS, FFN = 8, 2048
FB = FFN // BLK
FC = FFN // P
WB, WBLK = 2 * FB, KC * BLK
TOP_K = 2
TOKENS = TILES * P
SLOTS = (TOP_K * TOKENS + EXPERTS * (P - 1)) // P
ROOM = TOKENS // P
PLACES = EXPERTS * ROOM + 1
SCALE = float(D) ** -0.5
EPS = 1e-5
MASKED = -9000000000000000.0
LIMIT = 2.0 ** 53
HUGE = 3.0e38
GUESS = float(0x5F3759DF)
NEWTON = 3

C_ID, C_TRI, C_ONE, C_ME, C_SPARE, C_EXP = 0, P, 2 * P, 3 * P, 3 * P + 1, 3 * P + 2
C_ROOM = C_EXP + EXPERTS
C_SLOT = C_ROOM + EXPERTS
C_END = C_SLOT + SLOTS * EXPERTS

LOADED_TURNED = 1
SUM_ORDER = [NBLK - 1] + list(range(LOADED_TURNED, NBLK - 1)) + list(range(LOADED_TURNED))
TURN_ORDER = [NBLK - 1] + list(range(LOADED_TURNED, NBLK - 1))
FILLS_BLK = {b: 2 * KC if b < NBLK - 1 else 2 for b in TURN_ORDER}
FIRST_FILL = {b: 1 + sum(FILLS_BLK[c] for c in TURN_ORDER[:n]) for n, b in enumerate(TURN_ORDER)}
QK_FILLS = 1 + sum(FILLS_BLK.values())
P_FILLS = -(-CHUNKS // 4)
FILLS = QK_FILLS + P_FILLS
BANKS = 3


def by_act(r):
    return r % 3 != 2


def upto(r, act):
    return sum(by_act(x) == act for x in range(r + 1))


def count_at(j, r, n_qk, n_all, n_r):
    if isinstance(j, int) and j == -1:
        return n_r
    if isinstance(j, int) and j == TILES - 1:
        return n_all * j + n_r
    return j * n_all + (n_qk + n_r)


def filled_at(j, r):
    return count_at(j, r, QK_FILLS, FILLS, r + 1)


def copied_at(j, r):
    act = by_act(r)
    return act, count_at(j, r, upto(QK_FILLS - 1, act), upto(FILLS - 1, act), upto(r, act))


def bank_before(j, r):
    last = isinstance(j, int) and j == TILES - 1
    if r >= BANKS and not (last and r < QK_FILLS + BANKS):
        return j, r - BANKS
    if isinstance(j, int) and j == -1:
        return None
    top = QK_FILLS if isinstance(j, int) and j == 0 else FILLS
    return j - 1, max(x for x in range(top) if x % BANKS == r % BANKS)


class Steps:

    def __init__(self, engine, semaphore):
        self.engine, self.semaphore, self.before, self.n = engine, semaphore, 0, 0

    def then_next(self, instruction):
        instruction.then_inc(self.semaphore, 1)
        self.n += 1
        self.engine.wait_ge(self.semaphore, self.before + self.n)

    def enter(self, turn, per_turn):
        self.start = self.before + self.n
        self.before, self.n, self.per_turn = turn * per_turn + self.start, 0, per_turn

    def leave(self, turns):
        assert self.n == self.per_turn, self.n
        self.before, self.n = self.start + turns * self.per_turn, 0


def build(nc, x, ctx_in, ctx_turned, mask, gamma, beta, w_qkv, w_out, w_router, w1, w2, consts, acc):
    tokens_x = nc.dram_tensor("tokens_x", (TOKENS + P, D), F32, kind="Internal").ap()
    slots_m = nc.dram_tensor("slots_m", (PLACES * P, 2), F32, kind="Internal").ap()

    with ExitStack() as stack:
        def sb(name, shape, dt=F32):
            return stack.enter_context(nc.sbuf_tensor(name, shape, dt))

        def sem(name):
            return stack.enter_context(nc.semaphore(name))

        res = sb("res", [P, TILES * D])
        cst = sb("cst", [P, C_END])
        small = sb("small", [P, 64])
        route = sb("route", [P, 1100])
        zeros = sb("zeros", [P, D])
        nobody = sb("nobody", [P, PLACES, 2])
        with nc.sbuf_tensor("arena", [P, 44358 + 2 * KC * T_REST], F32) as arena:
            pass
        with ExitStack() as given_back:
            def lay(name, shape, dt):
                return given_back.enter_context(nc.sbuf_tensor(name, shape, dt))

            lay("before_vo", [P, 4096], F32)
            with nc.sbuf_tensor("vo_raw", [P, 2, WBLK], F32) as vo_raw:
                pass
            vo_low = lay("vo_low", [P, 2, WBLK], F32R)
            vo_high = lay("vo_high", [P, 2, WBLK], F32R)
            lay("before_parts", [P, 37248 - 12288], F32)
            xn_parts = lay("xn_parts", [P, 2, 2, KC, P], F32R)
            c_parts = lay("c_parts", [P, 2, KC, P], F32R)
        with nc.sbuf_tensor("before_w", [P, 13312], F32), nc.sbuf_tensor("w_raw_space", [P, WB, WBLK], F32) as w_raw_space:
            pass
        low_space = sb("low_space", [P, 12288], F32R)
        rows_space = sb("rows_space", [P, 2 * D])
        w_low = sb("w_low", [P, WB, WBLK], F32R)
        h_parts = sb("h_parts", [P, 2, FC, P], F32R)
        hid = sb("hid", [P, FFN])
        yb_space = sb("yb_space", [P, 2 * D])
        sb("gap", [P, 384])
        mid_space = sb("mid_space", [P, 6144], F32R)

        def view(at, *dims):
            n = 1
            for d in dims:
                n *= d
            a = arena[:, at:at + n]
            if len(dims) == 2:
                a = a.rearrange("p (a b) -> p a b", a=dims[0])
            if len(dims) == 3:
                a = a.rearrange("p (a b c) -> p a b c", a=dims[0], b=dims[1])
            return a

        ident = cst[:, C_ID:C_ID + P]
        before_me = cst[:, C_TRI:C_TRI + P]
        ones = cst[:, C_ONE:C_ONE + P]
        me = cst[:, C_ME:C_ME + 1]
        spare = cst[:, C_SPARE:C_SPARE + 1]
        expert_key = cst[:, C_EXP:C_EXP + EXPERTS]
        room_at = cst[:, C_ROOM:C_ROOM + EXPERTS]
        slot_no = cst[:, C_SLOT:C_END].rearrange("p (s e) -> p s e", e=EXPERTS)

        ctxb = [view(i * 2 * CHUNKS * D, 2, CHUNKS, D) for i in range(2)]
        ctxT = [view(26624 + i * 4096, 2, KC, BLK) for i in range(2)]
        ctxT_rest = view(44358, 2, KC, T_REST)
        mask_sb = arena[:, 34816:34816 + T].bitcast(I32)
        bound = arena[:, 36418:36418 + T]
        prob = arena[:, 38020:38020 + T]
        probT = view(39622, CHUNKS, P)
        xqT = [view(41286 + i * D, KC, P) for i in range(2)]
        xq = arena[:, 42310:42310 + D]
        att = arena[:, 42822:42822 + D]
        gam = arena[:, 43334:43334 + D]
        bet = arena[:, 43846:43846 + D]
        wqk_sb = view(0, 2, KC, D)
        rw_sb = view(12288, KC, EXPERTS)
        SELF = 29696
        xn = [arena[:, SELF + i * D:SELF + (i + 1) * D] for i in range(2)]
        xnT = [view(SELF + (2 + i) * D, KC, P) for i in range(2)]
        qT = [view(SELF + (4 + i) * D, KC, P) for i in range(2)]
        kT = [view(SELF + (6 + i) * D, KC, P) for i in range(2)]
        vv = [arena[:, SELF + (8 + i) * D:SELF + (9 + i) * D] for i in range(2)]
        xr = [arena[:, SELF + (10 + i) * D:SELF + (11 + i) * D] for i in range(2)]
        xrT = view(SELF + 13 * D, KC, P)
        pr = [arena[:, SELF + 14 * D + i * P:SELF + 14 * D + (i + 1) * P] for i in range(2)]
        prT = arena[:, SELF + 14 * D + 2 * P:SELF + 14 * D + 3 * P]
        xg = [rows_space[:, i * D:(i + 1) * D] for i in range(2)]
        yb = [yb_space[:, i * D:(i + 1) * D] for i in range(2)]

        def flat(tensor, at_):
            return tensor[:, at_:at_ + WBLK]

        w_raw = [w_raw_space[:, b, :] for b in range(WB)]
        w_high = ([flat(low_space, 8192 + b * WBLK) for b in range(2)] + [flat(mid_space, b * WBLK) for b in range(3)]
                  + [flat(low_space, b * WBLK) for b in range(3)])
        xT_parts = [[low_space[:, 6144 + (2 * i + part) * D:6144 + (2 * i + part + 1) * D]
                     .rearrange("p (k t) -> p k t", k=KC) for part in range(2)] for i in range(2)]

        stats, mv, rstd = small[:, 0:6], small[:, 6:8], small[:, 8:9]
        var, half = small[:, 9:10], small[:, 18:19]
        top, negtop = small[:, 10:11], small[:, 12:14]
        rowsum, inv = small[:, 14:16], small[:, 16:17]

        at = [0]

        def rt(*dims):
            n = dims[0] * (dims[1] if len(dims) == 2 else 1)
            a = route[:, at[0]:at[0] + n]
            at[0] += n
            return a.rearrange("p (a b) -> p a b", a=dims[0]) if len(dims) == 2 else a

        logit, logit2, tmp, rank = rt(EXPERTS), rt(EXPERTS), rt(EXPERTS), rt(EXPERTS)
        picks = [rt(TOP_K, EXPERTS) for _ in range(2)]
        pick = [[both_picks[:, n, :] for n in range(TOP_K)] for both_picks in picks]
        ranked = rt(TOP_K, EXPERTS)
        both = [rt(EXPERTS) for _ in range(2)]
        cum = [rt(EXPERTS) for _ in range(2)]
        best, low, posf, token = rt(TOP_K), rt(1), rt(TOP_K), rt(1)
        ratio = [rt(1) for _ in range(2)]
        pos = [rt(TOP_K).bitcast(I32) for _ in range(2)]
        meta = [rt(TOP_K, 2) for _ in range(2)]
        meta_i = [m.bitcast(I32) for m in meta]
        ahead = [rt(2) for _ in range(2)]
        gm = [rt(2) for _ in range(2)]
        cnt_i, cnt_r = rt(EXPERTS).bitcast(I32), rt(EXPERTS).bitcast(I32)
        lots, ends = rt(EXPERTS), rt(EXPERTS + 1)
        past, before_f, weighed = rt(SLOTS, EXPERTS), rt(SLOTS), rt(SLOTS, EXPERTS)
        taken, slot_f = rt(SLOTS), rt(SLOTS)
        used = rt(1).bitcast(I32)
        slot_e, slot_at = rt(SLOTS).bitcast(I32), rt(SLOTS).bitcast(I32)

        ps = stack.enter_context(nc.psum_tensor("ps", [P, 8 * BLK], F32))

        def bank(i, n=1):
            return ps[:, i * BLK:(i + n) * BLK]

        x_in, x1_in, x_rest_in, cst_in, gb_in = sem("x_in"), sem("x1_in"), sem("x_rest_in"), sem("cst_in"), sem("gb_in")
        ctx_here = [[sem(f"ctx_here{i}_{b}") for b in range(NBLK)] for i in range(2)]
        ctxT_here = [sem(f"ctxT_here{b}") for b in range(LOADED_TURNED)]
        mask_in = sem("mask_in")
        v_own, p_own = sem("v_own"), sem("p_own")
        xq_ready = sem("xq_ready")
        filled = sem("filled")
        copied = {True: sem("copied_by_act"), False: sem("copied_by_dve")}
        scored = sem("scored")
        bound_ready = sem("bound_ready")
        masked = sem("masked")
        negtop_ready = sem("negtop_ready")
        exp_done = sem("exp_done")
        pv_block = sem("pv_block")
        att_read = sem("att_read")
        att_ready = sem("att_ready")
        res1 = sem("res1")

        vo_in = [sem(f"vo_in{i}") for i in range(2)]
        vo_high_ready, vo_ready = sem("vo_high_ready"), sem("vo_ready")
        xn_high_ready, xn_parts_ready = sem("xn_high_ready"), sem("xn_parts_ready")
        w_in, zero_set, zero_out = sem("w_in"), sem("zero_set"), sem("zero_out")
        pr_clear = sem("pr_clear")
        xn_ready = sem("xn_ready")
        t1_done, t1_copied = sem("t1_done"), sem("t1_copied")
        q_done, q_copied = sem("q_done"), sem("q_copied")
        k_done, k_copied = sem("k_done"), sem("k_copied")
        v_done, v_copied = sem("v_done"), sem("v_copied")
        s_done, top_ready, e_done, pr_ready = sem("s_done"), sem("top_ready"), sem("e_done"), sem("pr_ready")
        pt_done, pt_copied = sem("pt_done"), sem("pt_copied")
        ct_done, ct_copied = sem("ct_done"), sem("ct_copied")
        o_done, res2 = sem("o_done"), sem("res2")
        xn2_ready = sem("xn2_ready")
        t2_done, t2_copied = sem("t2_done"), sem("t2_copied")
        r_done = sem("r_done")

        ranks_read = sem("ranks_read")
        picked, ratio_ready = sem("picked"), sem("ratio_ready")
        rank_done, pos_ready = sem("rank_done"), sem("pos_ready")
        sent, acc_set = sem("sent"), sem("acc_set")
        count_done, slot_ready = sem("count_done"), sem("slot_ready")

        places_free = sem("places_free")
        x_out = [sem(f"x_out{i}") for i in range(2)]
        gate_ready, row_steps = sem("gate_ready"), sem("row_steps")
        m_here = [sem(f"m_here{i}") for i in range(2)]
        x_here = [sem(f"x_here{i}") for i in range(2)]
        raw_here = [sem(f"raw_here{b}") for b in range(WB)]
        w_high_ready, w_ready = sem("w_high_ready"), sem("w_ready")
        x_turned, x_high_ready, x_ready = sem("x_turned"), sem("x_high_ready"), sem("x_ready")
        up_done, gelu_done = sem("up_done"), sem("gelu_done")
        h_turned, h_high_ready, h_ready = sem("h_turned"), sem("h_high_ready"), sem("h_ready")
        down_done, y_ready = sem("down_done"), sem("y_ready")
        added = [sem(f"added{i}") for i in range(2)]

        block = stack.enter_context(nc.Block())

        def in_use(eng):
            return eng.value_load(used[0:1, :], min_val=EXPERTS, max_val=SLOTS)

        def load_block(eng, e, b):
            w, n = (w1, b) if b < FB else (w2, b - FB)
            eng.dma_start(w_raw[b], w[bass.ds(e, 1), :, n * WBLK:(n + 1) * WBLK].rearrange("o p n -> p (o n)")
                          ).then_inc(raw_here[b], 16)

        def tile_of(j):
            return res[:, bass.ds(j * D, D)]

        def carry_waits(dve):
            dve.memset(small[:, 20:21], 0.0)

        def carry_pool_waits(pool, own, column=22):
            if not isinstance(own.before, int) or own.before + own.n >= 1:
                pool.wait_ge(own.semaphore, own.before + own.n)
            pool.tensor_tensor(small[:, column:column + 1], small[:, 21:22], small[:, 21:22], ALU.add
                               ).then_inc(own.semaphore, 1)
            own.n += 1

        def place(eng, j, p, par, r):
            o = bank(NBLK + r % BANKS)
            copy = eng.copy if by_act(r) else eng.tensor_copy
            if r == 0:
                return eng.mul(xqT[par], o.rearrange("p (k t) -> p k t", k=KC), SCALE)
            if r >= QK_FILLS:
                c = 4 * SUM_ORDER[r - QK_FILLS]
                if r < QK_FILLS + 2 and not (isinstance(j, int) and j == 0):
                    eng.wait_ge(pv_block, j * NBLK)
                if c + 4 <= CHUNKS:
                    return copy(probT[:, c:c + 4, :], o.rearrange("p (c q) -> p c q", c=4))
                return copy(probT[0:T_REST, c, :], o[0:T_REST, 0:P])
            blk = max(TURN_ORDER, key=lambda b: FIRST_FILL[b] if FIRST_FILL[b] <= r else -1)
            n = r - FIRST_FILL[blk]
            if blk == NBLK - 1:
                if n == 0 and not (isinstance(p, int) and p == 0):
                    eng.wait_ge(scored, p * NBLK)
                return copy(ctxT_rest[:, n, :, :], o.rearrange("p (k t) -> p k t", k=KC)[:, :, 0:T_REST])
            if n < 2 and not (isinstance(p, int) and p == 0 and blk < 2):
                eng.wait_ge(scored, p * NBLK + (blk - 1))
            return copy(ctxT[blk % 2][:, n // KC, n % KC, :], o)

        @block.sync
        def _(sp):
            def load_ctx(p, par, blks=SUM_ORDER):
                for blk in blks:
                    if not (isinstance(p, int) and p < 2):
                        sp.wait_ge(pv_block, p * NBLK + (SUM_ORDER.index(blk) + 1 - 2 * NBLK))
                        if blk == 0:
                            sp.wait_ge(bound_ready, p)
                            load_mask(p)
                    for b in range(2):
                        src = ctx_in[bass.ds(2 * p + b, 1), :, :]
                        if blk < NBLK - 1:
                            sp.dma_start(ctxb[par][:, b, 4 * blk:4 * blk + 4, :],
                                         src[:, blk * BLK:(blk + 1) * BLK, :].rearrange("o (c p) d -> p (o c) d", p=P)
                                         ).then_inc(ctx_here[par][blk], 16)
                        else:
                            sp.dma_start(ctxb[par][0:T_REST, b, CHUNKS - 1, :],
                                         src[:, (CHUNKS - 1) * P:T, :].rearrange("o p d -> p (o d)")
                                         ).then_inc(ctx_here[par][blk], 16)

            def load_turned(p, blk):
                if not (isinstance(p, int) and p == 0):
                    sp.wait_ge(scored, p * NBLK - 1)
                for b in range(2):
                    sp.dma_start(ctxT[blk][:, b, :, :],
                                 ctx_turned[bass.ds(2 * p + b, 1), :, LOADED_TURNED - 1 - blk, :, :]
                                 .rearrange("o p k n -> p (o k) n")).then_inc(ctxT_here[blk], 16)

            def load_mask(p):
                sp.dma_start(mask_sb, mask[bass.ds(p * P, P), :]).then_inc(mask_in, 16)

            sp.dma_start(res[:, 0:D], x[0:P, :]).then_inc(x_in, 16)
            sp.dma_start(cst[:], consts).then_inc(cst_in, 16)
            load_ctx(0, 0, [NBLK - 1])
            load_ctx(0, 0, [1])
            load_turned(0, 0)
            load_ctx(0, 0, [2])
            sp.dma_start(res[:, D:2 * D], x[P:2 * P, :]).then_inc(x1_in, 16)
            load_mask(0)
            load_ctx(1, 1, [NBLK - 1, 1])
            load_turned(1, 0)
            load_ctx(1, 1, [2])
            sp.wait_ge(bound_ready, 1)
            load_mask(1)
            sp.dma_start(res[:, 2 * D:].rearrange("p (t d) -> p t d", d=D),
                         x[2 * P:, :].rearrange("(t p) d -> p t d", p=P)).then_inc(x_rest_in, 16)
            load_ctx(0, 0, [0])
            sp.dma_start(gam, gamma.partition_broadcast(P)).then_inc(gb_in, 16)
            sp.dma_start(bet, beta.partition_broadcast(P)).then_inc(gb_in, 16)
            load_ctx(1, 1, [0])
            with sp.Fori(1, TILES // 2) as h:
                for par in range(2):
                    p = h * 2 + par
                    load_turned(p, 0)
                    load_ctx(p, par)
            sp.wait_ge(pv_block, NBLK * (TILES - 1))
            sp.dma_start(wqk_sb, w_qkv[:, 0:2 * WBLK].rearrange("p (j k h) -> p j k h", j=2, k=KC)).then_inc(w_in, 16)
            sp.dma_start(vo_raw[:, 0, :], w_qkv[:, 2 * WBLK:]).then_inc(vo_in[0], 16)
            sp.dma_start(vo_raw[:, 1, :], w_out).then_inc(vo_in[1], 16)
            sp.dma_start(rw_sb, w_router.rearrange("p (k e) -> p k e", k=KC)).then_inc(w_in, 16)
            sp.wait_ge(zero_set, 2)
            sp.dma_start(slots_m.rearrange("(s p) d -> p s d", p=P), nobody[:]).then_inc(zero_out, 16)
            sp.dma_start(tokens_x[TOKENS:TOKENS + P, :], zeros[:]).then_inc(zero_out, 16)
            sp.dma_start(acc[TOKENS:TOKENS + P, :], zeros[:]).then_inc(acc_set, 16)
            sp.wait_ge(pv_block, NBLK * TILES)
            for b in range(WB):
                load_block(sp, 0, b)
            with sp.Fori(0, TILES // 2) as h:
                for par in range(2):
                    t = h * 2 + par
                    sp.wait_ge(res2, t + 1)
                    sp.dma_start(acc[bass.ds(t * P, P), :], tile_of(t)).then_inc(acc_set, 16)
                    sp.wait_ge(xn2_ready, t + 1)
                    sp.dma_start(tokens_x[bass.ds(t * P, P), :], xr[par]).then_inc(x_out[par], 16)
            sp.wait_ge(acc_set, 16 * (TILES + 1))
            for par in range(2):
                sp.wait_ge(x_out[par], 16 * (TILES // 2))

        @block.gpsimd
        def _(pool):
            own = Steps(pool, p_own)

            def bounds(p):
                pool.wait_ge(mask_in, p * 16 + 16)
                if not (isinstance(p, int) and p == 0):
                    pool.wait_ge(masked, p * 2)
                carry_pool_waits(pool, own)
                pool.tensor_scalar(bound, mask_sb, 0, MASKED - LIMIT, ALU.is_equal, ALU.mult).then_inc(bound_ready, 1)

            def residual(j):
                pool.wait_ge(att_ready, j + 1)
                own.then_next(pool.tensor_tensor(att, att, gam, ALU.mult))
                own.then_next(pool.tensor_tensor(att, att, bet, ALU.add))
                pool.tensor_tensor(tile_of(j), tile_of(j), att, ALU.add).then_inc(res1, 1)

            own.then_next(pool.memset(small[:, 21:22], 0.0))
            bounds(0)
            bounds(1)
            pool.wait_ge(gb_in, 32)
            with pool.Fori(0, TILES - 2) as j:
                own.enter(j, 3)
                bounds(j + 2)
                residual(j)
                own.leave(TILES - 2)
            residual(TILES - 2)
            residual(TILES - 1)

            def send(t, par):
                pool.wait_ge(pos_ready, t + 1)
                pool.wait_ge(places_free, t + TOP_K)
                carry_pool_waits(pool, own)
                for n in range(TOP_K):
                    where = bass.IndirectOffsetOnAxis(ap=pos[par][:, n:n + 1], axis=0)
                    pool.indirect_dma_start(out=slots_m, out_offset=where, in_=meta[par][:, n, :], in_offset=None
                                            ).then_inc(sent, 16)
                pool.wait_ge(sent, t * (16 * TOP_K) + 16 * TOP_K)
                pool.tensor_tensor(small[:, 23:24], small[:, 21:22], small[:, 21:22], ALU.add).then_inc(places_free, 1)

            for n in range(2):
                pool.memset(small[:, 24 + n:25 + n], 0.0).then_inc(places_free, 1)
            pool.wait_ge(zero_out, 32)
            with pool.Fori(0, TILES // 2) as h:
                own.enter(h, 2)
                for par in range(2):
                    send(h * 2 + par, par)
                own.leave(TILES // 2)

            rows = Steps(pool, row_steps)

            def fetch(i, h, par):
                row = 0 if isinstance(i, int) and i == 0 else pool.value_load(
                    slot_at[0:1, bass.ds(i, 1)], min_val=0, max_val=(PLACES - 1) * P)
                if not (isinstance(i, int) and i < 2):
                    pool.wait_ge(gate_ready, i - 1)
                    pool.wait_ge(x_turned, i - 1)
                pool.dma_start(ahead[par], slots_m[bass.ds(row, P), :]).then_inc(m_here[par], 16)
                pool.wait_ge(m_here[par], h * 16 + 16)
                carry_pool_waits(pool, rows, 27)
                pool.indirect_dma_start(
                    out=xg[par], out_offset=None, in_=tokens_x,
                    in_offset=bass.IndirectOffsetOnAxis(ap=ahead[par].bitcast(I32)[:, 1:2], axis=0)
                ).then_inc(x_here[par], 16)
                pool.wait_ge(x_here[par], h * 16 + 16)

            def keep(par):
                carry_pool_waits(pool, own)
                pool.tensor_copy(gm[par].bitcast(I32), ahead[par].bitcast(I32)).then_inc(gate_ready, 1)

            def add(i, h, par):
                pool.wait_ge(gate_ready, i + 1)
                pool.wait_ge(y_ready, i + 1)
                carry_pool_waits(pool, own)
                pool.indirect_dma_start(
                    out=acc, out_offset=bass.IndirectOffsetOnAxis(ap=gm[par].bitcast(I32)[:, 1:2], axis=0),
                    in_=yb[par], in_offset=None, compute_op=ALU.add).then_inc(added[par], 16)
                pool.wait_ge(added[par], h * 16 + 16)

            def slot(i, h, par):
                static = isinstance(i, int)
                if not static or i + 2 < SLOTS:
                    with pool.If(in_use(pool) > i + 1):
                        fetch(i + 2, h + 1, par)
                with pool.If(in_use(pool) > i):
                    add(i, h, par)
                    if not static or i + 2 < SLOTS:
                        keep(par)

            for par in range(2):
                pool.wait_ge(x_out[par], 16 * (TILES // 2))
            fetch(0, 0, 0)
            keep(0)
            pool.wait_ge(slot_ready, 1)
            fetch(1, 0, 1)
            keep(1)
            pool.wait_ge(acc_set, 16 * (TILES + 1))
            slot(0, 0, 0)
            slot(1, 0, 1)
            with pool.Fori(1, SLOTS // 2 - 1) as h:
                own.enter(h - 1, 4)
                rows.enter(h - 1, 2)
                for par in range(2):
                    slot(h * 2 + par, h, par)
                own.leave(SLOTS // 2 - 2)
                rows.leave(SLOTS // 2 - 2)
            for i in range(SLOTS - 3, SLOTS):
                slot(i, i // 2, i % 2)

        @block.tensor
        def _(pe):
            tp = [bank(NBLK + n) for n in range(BANKS)]
            att_ps = bank(7)

            def open_fill(j, r):
                if (prev := bank_before(j, r)) is not None:
                    act, n = copied_at(*prev)
                    pe.wait_ge(copied[act], n)
                return tp[r % BANKS]

            def scores(p, par, j, blk):
                n = min(BLK, T - blk * BLK)
                if blk < LOADED_TURNED:
                    pe.wait_ge(ctxT_here[blk], p * 32 + 32)
                else:
                    last = FIRST_FILL[blk] + FILLS_BLK[blk] - 1
                    for by in (True, False):
                        r = max(r for r in range(last - BANKS + 1, last + 1) if by_act(r) == by)
                        act, count = copied_at(j, r)
                        pe.wait_ge(copied[act], count)
                if blk == 0 and not (isinstance(p, int) and p == 0):
                    pe.wait_ge(masked, p * 2)
                for k in range(KC):
                    for b in range(2):
                        mm = pe.matmul(ps[64 * b:64 * b + 64, blk * BLK:blk * BLK + n],
                                       xqT[par][:, k, 64 * b:64 * b + 64],
                                       ctxT[blk % 2][:, b, k, :] if blk < NBLK - 1 else ctxT_rest[:, b, k, :],
                                       start=(k == 0), stop=(k == KC - 1))
                mm.then_inc(scored, 1)

            def qk(p, h, par, j):
                pe.wait_ge(xq_ready, p + 1)
                o = open_fill(j, 0)
                for k in range(KC):
                    mm = pe.transpose(o[:, k * P:(k + 1) * P], xq[:, k * P:(k + 1) * P], ident)
                mm.then_inc(filled, 1)
                turn_ctx(h, par, j, NBLK - 1)
                turn_ctx(h, par, j, 1)
                for blk in range(NBLK):
                    if blk == 0:
                        act, count = copied_at(j, 0)
                        pe.wait_ge(copied[act], count)
                    scores(p, par, j, blk)
                    if blk == 0:
                        turn_ctx(h, par, j, 2)

            def turn_ctx(h, par, j, blk):
                pe.wait_ge(ctx_here[par][blk], h * 32 + 32)
                r = FIRST_FILL[blk]
                for b in range(2):
                    for k in range(KC):
                        if blk < NBLK - 1 or k == 0:
                            o = open_fill(j, r)
                        if blk < NBLK - 1:
                            for c in range(4):
                                mm = pe.transpose(o[:, c * P:(c + 1) * P],
                                                  ctxb[par][:, b, 4 * blk + c, k * P:(k + 1) * P], ident)
                        else:
                            mm = pe.transpose(o[:, k * P:k * P + T_REST],
                                              ctxb[par][0:T_REST, b, CHUNKS - 1, k * P:(k + 1) * P],
                                              ident[0:T_REST, 0:T_REST])
                        if blk < NBLK - 1 or k == KC - 1:
                            mm.then_inc(filled, 1)
                            r += 1

            def pv(j, h, par):
                pe.wait_ge(exp_done, j + 1)
                for n, blk in enumerate(SUM_ORDER):
                    o = open_fill(j, QK_FILLS + n)
                    for c in range(4 * blk, min(4 * blk + 4, CHUNKS)):
                        m = P if c < CHUNKS - 1 else T_REST
                        mm = pe.transpose(o[0:m, (c % 4) * P:(c % 4 + 1) * P], prob[:, c * P:c * P + m], ident)
                    mm.then_inc(filled, 1)
                if not (isinstance(j, int) and j == 0):
                    pe.wait_ge(att_read, j)
                for n, blk in enumerate(SUM_ORDER):
                    act, count = copied_at(j, QK_FILLS + n)
                    pe.wait_ge(copied[act], count)
                    if blk < LOADED_TURNED:
                        pe.wait_ge(ctx_here[par][blk], h * 32 + 32)
                    chunks = range(4 * blk, min(4 * blk + 4, CHUNKS))
                    for c in chunks:
                        m = P if c < CHUNKS - 1 else T_REST
                        for b in range(2):
                            mm = pe.matmul(att_ps[64 * b:64 * b + 64, :], probT[0:m, c, 64 * b:64 * b + 64],
                                           ctxb[par][0:m, b, c, :], start=(n == 0 and c == chunks[0]),
                                           stop=(n == NBLK - 1 and c == chunks[-1]))
                    mm.then_inc(pv_block, 1)

            pe.wait_ge(cst_in, 16)
            qk(0, 0, 0, -1)
            qk(1, 0, 1, 0)
            pv(0, 0, 0)
            with pe.Fori(0, TILES // 2 - 1) as h:
                for par in range(2):
                    j = h * 2 + (1 + par)
                    qk(j + 1, h + 1, par, j)
                    pv(j, h + par, 1 - par)
            pv(TILES - 1, TILES // 2 - 1, 1)

            S, TB, QB, KB, VB, MB, CB, OB = (bank(n) for n in range(8))

            def product(out, rows, high, low, k, start, stop):
                high, low = high[:, k * BLK:(k + 1) * BLK], low[:, k * BLK:(k + 1) * BLK]
                pe.matmul(out, rows[0], high, start=start, stop=False)
                pe.matmul(out, rows[0], low, start=False, stop=False)
                return pe.matmul(out, rows[1], high, start=False, stop=stop)

            def turn_first(j, par):
                pe.wait_ge(xn_ready, j + 1)
                for k in range(KC):
                    mm = pe.transpose(TB[:, k * P:(k + 1) * P], xn[par][:, k * P:(k + 1) * P], ident)
                mm.then_inc(t1_done, 1)

            def project(j, par, which, dst, copied_out, done, hcs=range(KC)):
                if 0 in hcs:
                    pe.wait_ge(t1_copied, j + 1)
                    if not isinstance(j, int) or j >= 1:
                        pe.wait_ge(copied_out, j)
                for hc in hcs:
                    for k in range(KC):
                        mm = pe.matmul(dst[:, hc * P:(hc + 1) * P], wqk_sb[:, which, k, hc * P:(hc + 1) * P],
                                       xnT[par][:, k, :], start=(k == 0), stop=(k == KC - 1))
                if KC - 1 in hcs:
                    mm.then_inc(done, 1)

            def values(j, par):
                if not isinstance(j, int) or j >= 1:
                    pe.wait_ge(v_copied, j)
                if isinstance(j, int) and j == 0:
                    pe.wait_ge(vo_ready, 1)
                pe.wait_ge(xn_parts_ready, j + 1)
                for k in range(KC):
                    mm = product(VB, [xn_parts[:, par, part, k, :] for part in range(2)], vo_high[:, 0, :],
                                 vo_low[:, 0, :], k, k == 0, k == KC - 1)
                mm.then_inc(v_done, 1)

            def own_scores(j, par):
                pe.wait_ge(q_copied, j + 1)
                pe.wait_ge(k_copied, j + 1)
                if not isinstance(j, int) or j >= 1:
                    pe.wait_ge(e_done, j)
                if not isinstance(j, int) or j >= 2:
                    pe.wait_ge(ranks_read, j - 1)
                for k in range(KC):
                    mm = pe.matmul(S[:, 0:P], qT[par][:, k, :], kT[par][:, k, :], start=(k == 0), stop=(k == KC - 1))
                mm.then_inc(s_done, 1)

            def turn_probs(j, par):
                pe.wait_ge(pr_ready, j + 1)
                pe.transpose(MB[:, 0:P], pr[par], ident).then_inc(pt_done, 1)

            def weigh(j, par):
                pe.wait_ge(pt_copied, j + 1)
                pe.wait_ge(v_copied, j + 1)
                if not isinstance(j, int) or j >= 1:
                    pe.wait_ge(ct_copied, j)
                for hc in range(KC):
                    mm = pe.matmul(CB[:, hc * P:(hc + 1) * P], vv[par][:, hc * P:(hc + 1) * P], prT,
                                   start=True, stop=True)
                mm.then_inc(ct_done, 1)

            def project_out(j):
                pe.wait_ge(ct_copied, j + 1)
                if not isinstance(j, int) or j >= 1:
                    pe.wait_ge(res2, j)
                else:
                    pe.wait_ge(vo_ready, 2)
                for hc in range(KC):
                    mm = product(OB, [c_parts[:, part, hc, :] for part in range(2)], vo_high[:, 1, :], vo_low[:, 1, :],
                                 hc, hc == 0, hc == KC - 1)
                mm.then_inc(o_done, 1)

            def turn_second(j, par, first):
                pe.wait_ge(xn2_ready, j + 1)
                pe.wait_ge(t1_copied, first)
                for k in range(KC):
                    mm = pe.transpose(TB[:, k * P:(k + 1) * P], xr[par][:, k * P:(k + 1) * P], ident)
                mm.then_inc(t2_done, 1)

            def router(j):
                pe.wait_ge(t2_copied, j + 1)
                for k in range(KC):
                    mm = pe.matmul(MB[:, P:P + EXPERTS], xrT[:, k, :], rw_sb[:, k, :],
                                   start=(k == 0), stop=(k == KC - 1))
                mm.then_inc(r_done, 1)

            def ranks(j, par):
                pe.wait_ge(picked, j + 1)
                pe.matmul(S[:, P:P + EXPERTS], before_me, both[par], start=True, stop=False)
                pe.matmul(S[:, P:P + EXPERTS], ones, cum[par], start=False, stop=True).then_inc(rank_done, 1)

            def tile_step(j, par, front, back, back2, late=False):
                if front:
                    turn_first(j + 1, 1 - par)
                own_scores(j, par)
                if front:
                    project(j + 1, 1 - par, 0, QB, q_copied, q_done)
                    project(j + 1, 1 - par, 1, KB, k_copied, k_done, range(2))
                if back:
                    turn_second(j - 1, 1 - par, j + 2 if front else TILES)
                turn_probs(j, par)
                if front:
                    project(j + 1, 1 - par, 1, KB, k_copied, k_done, range(2, KC))
                weigh(j, par)
                if back2:
                    ranks(j - 2, par)
                if back:
                    router(j - 1)
                if late:
                    project_out(j)
                if front:
                    values(j + 1, 1 - par)
                if not late:
                    project_out(j)

            pe.wait_ge(w_in, 32)
            turn_first(0, 0)
            project(0, 0, 0, QB, q_copied, q_done)
            project(0, 0, 1, KB, k_copied, k_done)
            values(0, 0)
            pe.wait_ge(att_read, TILES)
            tile_step(0, 0, True, False, False)
            tile_step(1, 1, True, True, False)
            with pe.Fori(1, TILES // 2 - 1) as h:
                for par in range(2):
                    tile_step(h * 2 + par, par, True, True, True)
            tile_step(TILES - 2, 0, True, True, True, late=True)
            tile_step(TILES - 1, 1, False, True, True)
            pe.wait_ge(pos_ready, TILES - 2)
            ranks(TILES - 2, 0)
            turn_second(TILES - 1, 1, TILES)
            router(TILES - 1)
            pe.wait_ge(pos_ready, TILES - 1)
            ranks(TILES - 1, 1)
            pe.matmul(bank(6)[:, 0:EXPERTS], ones, cum[TILES % 2], start=True, stop=True).then_inc(count_done, 1)

            UB, HB, YB, XB = [bank(0), bank(1), bank(2)], [bank(3), bank(4)], [bank(5), bank(6)], bank(7)

            def turn_x(i, h, par):
                pe.wait_ge(x_here[par], h * 16 + 16)
                if not isinstance(i, int) or i >= 1:
                    pe.wait_ge(x_ready, i)
                for k in range(KC):
                    mm = pe.transpose(XB[:, k * P:(k + 1) * P], xg[par][:, k * P:(k + 1) * P], ident)
                mm.then_inc(x_turned, 1)

            def up(i, e, par, f):
                pe.wait_ge(w_ready, e * WB + (f + 1))
                if not (isinstance(i, int) and i == 0 and f < 3):
                    pe.wait_ge(gelu_done, i * FB + (f - 2))
                for k in range(KC):
                    mm = product(UB[f % 3], [part[:, k, :] for part in xT_parts[par]], w_high[f],
                                 w_low[:, f, :], k, k == 0, k == KC - 1)
                mm.then_inc(up_done, 1)

            def turn_h(i, f):
                pe.wait_ge(gelu_done, i * FB + (f + 1))
                if not (isinstance(i, int) and i == 0 and f < 2):
                    pe.wait_ge(h_ready, i * FB + (f - 1))
                for c in range(4):
                    mm = pe.transpose(HB[f % 2][:, c * P:(c + 1) * P], hid[:, f * BLK + c * P:f * BLK + (c + 1) * P], ident)
                mm.then_inc(h_turned, 1)

            def down(i, e, par, f):
                pe.wait_ge(h_ready, i * FB + (f + 1))
                pe.wait_ge(w_ready, e * WB + (FB + f + 1))
                for c in range(4):
                    mm = product(YB[par], [h_parts[:, part, 4 * f + c, :] for part in range(2)], w_high[FB + f],
                                 w_low[:, FB + f, :], c,
                                 f == 0 and c == 0, f == FB - 1 and c == 3)
                mm.then_inc(down_done, 1)

            def slot(i, h, par, last=False):
                e = 0 if isinstance(i, int) and i == 0 else pe.value_load(
                    slot_e[0:1, bass.ds(i, 1)], min_val=0, max_val=EXPERTS - 1)
                pe.wait_ge(x_ready, i + 1)
                up(i, e, par, 0)
                up(i, e, par, 1)
                turn_h(i, 0)
                up(i, e, par, 2)
                turn_h(i, 1)
                up(i, e, par, 3)
                turn_h(i, 2)
                if not isinstance(i, int) or i >= 2:
                    pe.wait_ge(y_ready, i - 1)
                down(i, e, par, 0)
                down(i, e, par, 1)
                turn_h(i, 3)
                if not last:
                    turn_x(i + 1, h + par, 1 - par)
                down(i, e, par, 2)
                down(i, e, par, 3)

            turn_x(0, 0, 0)
            slot(0, 0, 0)
            pe.wait_ge(slot_ready, 1)
            slot(1, 0, 1)
            slots_in_use = in_use(pe)
            with pe.Fori(1, SLOTS // 2) as h:
                for par in range(2):
                    with pe.If(slots_in_use > h * 2 + par):
                        slot(h * 2 + par, h, par)
            with pe.If(slots_in_use > SLOTS - 1):
                slot(SLOTS - 1, SLOTS // 2, 0, last=True)

        @block.scalar
        def _(act):
            def copy_out(j, p, par, r):
                act.wait_ge(filled, filled_at(j, r))
                place(act, j, p, par, r).then_inc(copied[True], 1)

            def qk_copies(j, p, par):
                for r in range(QK_FILLS):
                    if by_act(r):
                        copy_out(j, p, par, r)

            def exps(j, par):
                act.wait_ge(negtop_ready, j + 1)
                nc.scalar.activation(prob, prob, ACT.Exp, bias=negtop[:, par:par + 1], scale=1.0,
                                     accum_out=rowsum[:, par:par + 1]).then_inc(exp_done, 1)

            def p_copies(j):
                for r in range(QK_FILLS, FILLS):
                    if by_act(r):
                        copy_out(j, j, 0, r)

            act.wait_ge(cst_in, 16)
            qk_copies(-1, 0, 0)
            exps(0, 0)
            qk_copies(0, 1, 1)
            p_copies(0)
            with act.Fori(0, TILES // 2 - 1) as h:
                for par in range(2):
                    j = h * 2 + (1 + par)
                    exps(j, 1 - par)
                    qk_copies(j, j + 1, par)
                    p_copies(j)
            exps(TILES - 1, 1)
            p_copies(TILES - 1)

            def copy_t1(j, par):
                act.wait_ge(t1_done, j + 1)
                if not isinstance(j, int) or j >= 2:
                    act.wait_ge(v_done, j - 1)
                act.copy(xnT[par], bank(1).rearrange("p (k t) -> p k t", k=KC)).then_inc(t1_copied, 1)
                act.wait_ge(t1_copied, j + 1)
                act.copy(xn_parts[:, par, 0, :, :], xnT[par]).then_inc(xn_high_ready, 1)

            def copy_t2(j):
                act.wait_ge(t2_done, j + 1)
                if not isinstance(j, int) or j >= 1:
                    act.wait_ge(r_done, j)
                act.copy(xrT, bank(1).rearrange("p (k t) -> p k t", k=KC)).then_inc(t2_copied, 1)

            def copy_qkv(j, par, back=False):
                for n, (done, copied_out, dst) in enumerate(((q_done, q_copied, qT), (k_done, k_copied, kT),
                                                             (v_done, v_copied, vv))):
                    act.wait_ge(done, j + 1)
                    if not isinstance(j, int) or j >= 2:
                        act.wait_ge(s_done if n < 2 else ct_done, j - 1)
                    src = bank(2 + n)
                    if n < 2:
                        src = src.rearrange("p (k t) -> p k t", k=KC)
                    act.copy(dst[par], src).then_inc(copied_out, 1)
                    if back and n == 0:
                        copy_t2(j - 2)

            def own_exps(j, par):
                act.wait_ge(top_ready, j + 1)
                for b in range(2):
                    q = slice(64 * b, 64 * b + 64)
                    e = nc.scalar.activation(pr[par][q, 64 * b:64 * b + 64], bank(0)[q, 64 * b:64 * b + 64], ACT.Exp,
                                             bias=negtop[q, par:par + 1], scale=SCALE,
                                             accum_out=rowsum[q, par:par + 1])
                e.then_inc(e_done, 1)

            def gate_exp(j, par):
                act.wait_ge(picked, j + 1)
                nc.scalar.activation(ratio[par], ratio[par], ACT.Exp).then_inc(ratio_ready, 1)

            copy_t1(0, 0)
            for n in range(2):
                act.wait_ge(vo_in[n], 16)
                act.copy(vo_high[:, n, :], vo_raw[:, n, :]).then_inc(vo_high_ready, 1)
            copy_qkv(0, 0)
            act.wait_ge(pr_clear, 2)
            copy_t1(1, 1)
            own_exps(0, 0)
            copy_qkv(1, 1)
            copy_t1(2, 0)
            own_exps(1, 1)
            copy_qkv(2, 0, True)
            with act.Fori(1, TILES // 2 - 1) as h:
                for par in range(2):
                    j = h * 2 + par
                    copy_t1(j + 1, 1 - par)
                    own_exps(j, par)
                    gate_exp(j - 2, par)
                    copy_qkv(j + 1, 1 - par, True)
            for j in range(TILES - 2, TILES):
                if j + 1 < TILES:
                    copy_t1(j + 1, 1 - j % 2)
                own_exps(j, j % 2)
                gate_exp(j - 2, j % 2)
                if j + 1 < TILES:
                    copy_qkv(j + 1, 1 - j % 2, True)
                else:
                    copy_t2(j - 1)

            def split_high(e, b):
                act.wait_ge(raw_here[b], e * 16 + 16)
                act.copy(w_high[b], w_raw[b]).then_inc(w_high_ready, 1)

            def expert(i):
                return act.value_load(slot_e[0:1, bass.ds(i, 1)], min_val=0, max_val=EXPERTS - 1)

            def gelu(i, f):
                act.wait_ge(up_done, i * FB + (f + 1))
                if not (isinstance(i, int) and i == 0):
                    act.wait_ge(h_turned, i * FB + (f - FB + 1))
                nc.scalar.activation(hid[:, f * BLK:(f + 1) * BLK], bank(f % 3), ACT.Gelu).then_inc(gelu_done, 1)

            def high_h(i, f):
                act.wait_ge(h_turned, i * FB + (f + 1))
                if not (isinstance(i, int) and i == 0):
                    act.wait_ge(down_done, i * FB + (f - FB + 1))
                act.copy(h_parts[:, 0, 4 * f:4 * f + 4, :], bank(3 + f % 2).rearrange("p (c t) -> p c t", c=4)
                         ).then_inc(h_high_ready, 1)

            def high_x(i, par):
                act.wait_ge(x_turned, i + 1)
                act.copy(xT_parts[par][0], bank(7).rearrange("p (k t) -> p k t", k=KC)).then_inc(x_high_ready, 1)

            def slot(i, par, last=False):
                static = isinstance(i, int)
                e = 0 if static and i == 0 else expert(i)
                first = None if static and i == 0 else (e > expert(i - 1))
                after = None if last else expert(i + 1)

                def if_first(b):
                    if first is None:
                        split_high(e, b)
                    else:
                        with act.If(first):
                            split_high(e, b)

                gelu(i, 0)
                if_first(5)
                gelu(i, 1)
                if not last:
                    with act.If(after > e):
                        load_block(act, after, 0)
                        load_block(act, after, 1)
                high_h(i, 0)
                if_first(6)
                gelu(i, 2)
                high_h(i, 1)
                if_first(7)
                if not last:
                    with act.If(after > e):
                        load_block(act, after, 2)
                        split_high(after, 0)
                gelu(i, 3)
                high_h(i, 2)
                if not last:
                    with act.If(after > e):
                        load_block(act, after, 3)
                        split_high(after, 1)
                        act.wait_ge(down_done, i * FB + 1)
                        load_block(act, after, 4)
                high_h(i, 3)
                if not last:
                    high_x(i + 1, 1 - par)
                    with act.If(after > e):
                        for b in range(5, WB):
                            act.wait_ge(down_done, i * FB + (b - FB + 1))
                            load_block(act, after, b)
                            split_high(after, b - 3)

            act.wait_ge(o_done, TILES)
            for b in range(2):
                split_high(0, b)
            gate_exp(TILES - 2, 0)
            copy_t2(TILES - 1)
            gate_exp(TILES - 1, 1)
            act.wait_ge(res1, TILES)
            for b in range(2, 5):
                split_high(0, b)
            nc.scalar.activation(small[:, 26:27], half, ACT.Gelu)
            high_x(0, 0)
            act.wait_ge(slot_ready, 1)
            slot(0, 0)
            slot(1, 1)
            slots_in_use = in_use(act)
            with act.Fori(1, SLOTS // 2) as h:
                for par in range(2):
                    with act.If(slots_in_use > h * 2 + par):
                        slot(h * 2 + par, par)
            with act.If(slots_in_use > SLOTS - 1):
                slot(SLOTS - 1, 0, last=True)

        @block.vector
        def _(dve):
            own = Steps(dve, v_own)

            def rsqrt_start(v, variance):
                own.then_next(dve.tensor_scalar(v, variance, EPS, None, ALU.add))
                own.then_next(dve.tensor_scalar(rstd.bitcast(I32), v.bitcast(I32), -0.5, GUESS, ALU.mult, ALU.add))
                own.then_next(dve.tensor_scalar(v, v, -0.5, None, ALU.mult))

            def rsqrt_step(v):
                own.then_next(dve.scalar_tensor_tensor(out=half, in0=rstd, scalar=rstd, in1=v,
                                                       op0=ALU.mult, op1=ALU.mult))
                own.then_next(dve.scalar_tensor_tensor(out=rstd, in0=half, scalar=1.5, in1=rstd,
                                                       op0=ALU.add, op1=ALU.mult))

            def moments(src):
                carry_waits(dve)
                own.then_next(dve.bn_stats(stats, src))
                carry_waits(dve)
                own.then_next(dve.bn_aggr(mv, stats))

            NORM = 2 + 3 + 2 * NEWTON

            def normalize(dst, src):
                moments(src)
                rsqrt_start(var, mv[:, 1:2])
                for _ in range(NEWTON):
                    rsqrt_step(var)
                return dve.tensor_scalar(dst, src, mv[:, 0:1], rstd, ALU.subtract, ALU.mult)

            def queries(p):
                if not isinstance(p, int) or p >= 1:
                    dve.wait_ge(filled, filled_at(p - 2 if not isinstance(p, int) or p > 1 else -1, 0))
                normalize(xq, tile_of(p)).then_inc(xq_ready, 1)

            def softmax(j, par):
                dve.wait_ge(bound_ready, j + 1)
                if not isinstance(j, int) or j >= 1:
                    dve.wait_ge(filled, filled_at(j - 1, FILLS - 1))
                for n, (a, b) in enumerate(((0, 2 * BLK), (2 * BLK, T))):
                    dve.wait_ge(scored, j * NBLK + (2 * n + 2))
                    dve.scalar_tensor_tensor(out=prob[:, a:b], in0=bound[:, a:b], scalar=LIMIT, in1=ps[:, a:b],
                                             op0=ALU.add, op1=ALU.min).then_inc(masked, 1)
                dve.wait_ge(masked, j * 2 + 2)
                own.then_next(dve.tensor_reduce(top, prob, AX.X, ALU.max))
                dve.tensor_scalar(negtop[:, par:par + 1], top, -1.0, None, ALU.mult).then_inc(negtop_ready, 1)

            def attended(j, par):
                dve.wait_ge(pv_block, j * NBLK + NBLK)
                own.then_next(dve.reciprocal(inv, rowsum[:, par:par + 1]))
                if not isinstance(j, int) or j >= 1:
                    dve.wait_ge(res1, j)
                dve.tensor_scalar(att, bank(7), inv, None, ALU.mult).then_inc(att_read, 1)
                dve.wait_ge(att_read, j + 1)

            def attended_norm(part):
                if part == 0:
                    moments(att)
                if part == 1:
                    rsqrt_start(var, mv[:, 1:2])
                if 2 <= part < 2 + NEWTON:
                    rsqrt_step(var)
                if part == 2 + NEWTON:
                    dve.tensor_scalar(att, att, mv[:, 0:1], rstd, ALU.subtract, ALU.mult).then_inc(att_ready, 1)

            def copies(j, p, par, rs):
                for r in rs:
                    if not by_act(r):
                        dve.wait_ge(filled, filled_at(j, r))
                        place(dve, j, p, par, r).then_inc(copied[False], 1)

            dve.wait_ge(x_in, 16)
            queries(0)
            dve.memset(zeros[:], 0.0).then_inc(zero_set, 1)
            own.then_next(dve.memset(nobody[:, :, 0], 0.0))
            dve.wait_ge(cst_in, 16)
            dve.tensor_scalar(nobody[:, :, 1].bitcast(I32), nobody[:, :, 0], spare, None, ALU.add
                              ).then_inc(zero_set, 1)
            copies(-1, 0, 0, range(QK_FILLS))
            dve.wait_ge(x1_in, 16)
            queries(1)
            softmax(0, 0)
            copies(0, 1, 1, range(FILLS))
            dve.wait_ge(x_rest_in, 16)
            with dve.Fori(0, TILES // 2 - 1) as h:
                own.enter(h, 2 * (NORM + 1 + 1 + NORM))
                for par in range(2):
                    j = h * 2 + (1 + par)
                    queries(j + 1)
                    softmax(j, 1 - par)
                    copies(j, j + 1, par, range(4))
                    attended(j - 1, par)
                    for part in range(3 + NEWTON):
                        copies(j, j + 1, par, range(4 + 3 * part, min(7 + 3 * part, FILLS)))
                        attended_norm(part)
                    copies(j, j + 1, par, range(4 + 3 * (3 + NEWTON), FILLS))
                own.leave(TILES // 2 - 1)
            softmax(TILES - 1, 1)
            copies(TILES - 1, TILES - 1, 1, range(QK_FILLS, FILLS))
            attended(TILES - 2, 0)
            for part in range(3 + NEWTON):
                attended_norm(part)
            for i in range(2):
                dve.memset(pr[i], 0.0).then_inc(pr_clear, 1)

            def first_norm(j, par):
                dve.wait_ge(res1, j + 1)
                if not isinstance(j, int) or j >= 2:
                    dve.wait_ge(t1_done, j - 1)
                normalize(xn[par], tile_of(j)).then_inc(xn_ready, 1)

            def tops(j, par):
                dve.wait_ge(s_done, j + 1)
                for b in range(2):
                    q = slice(64 * b, 64 * b + 64)
                    own.then_next(dve.tensor_reduce(top[q, :], bank(0)[q, 64 * b:64 * b + 64], AX.X, ALU.max))
                dve.tensor_scalar(negtop[:, par:par + 1], top, -SCALE, None, ALU.mult).then_inc(top_ready, 1)

            def probs(j, par):
                dve.wait_ge(e_done, j + 1)
                own.then_next(dve.reciprocal(inv, rowsum[:, par:par + 1]))
                dve.tensor_scalar(pr[par], pr[par], inv, None, ALU.mult).then_inc(pr_ready, 1)

            def copy_pt(j):
                dve.wait_ge(pt_done, j + 1)
                if not isinstance(j, int) or j >= 1:
                    dve.wait_ge(ct_done, j)
                dve.tensor_copy(prT, bank(5)[:, 0:P]).then_inc(pt_copied, 1)

            def copy_ct(j):
                dve.wait_ge(ct_done, j + 1)
                if not isinstance(j, int) or j >= 1:
                    dve.wait_ge(o_done, j)
                src = bank(6).rearrange("p (k t) -> p k t", k=KC)
                own.then_next(dve.tensor_copy(c_parts[:, 0, :, :], src))
                dve.tensor_tensor(c_parts[:, 1, :, :], src, c_parts[:, 0, :, :].bitcast(F32), ALU.subtract
                                  ).then_inc(ct_copied, 1)

            def route_first(j, par):
                dve.wait_ge(r_done, j + 1)
                own.then_next(dve.tensor_copy(logit, bank(5)[:, P:P + EXPERTS]))
                src = logit
                for n in range(TOP_K):
                    own.then_next(dve.tensor_reduce(best[:, n:n + 1], src, AX.X, ALU.max))
                    own.then_next(dve.scalar_tensor_tensor(out=tmp, in0=src, scalar=best[:, n:n + 1], in1=expert_key,
                                                           op0=ALU.is_equal, op1=ALU.mult))
                    own.then_next(dve.tensor_reduce(low, tmp, AX.X, ALU.min))
                    own.then_next(dve.tensor_scalar(pick[par][n], tmp, low, None, ALU.is_equal))
                    if n == 0:
                        own.then_next(dve.scalar_tensor_tensor(out=logit2, in0=pick[par][0], scalar=-HUGE, in1=logit,
                                                               op0=ALU.mult, op1=ALU.add))
                        src = logit2
                own.then_next(dve.tensor_tensor(ratio[par], best[:, 1:2], best[:, 0:1], ALU.subtract))
                own.then_next(dve.tensor_tensor(both[par], pick[par][0], pick[par][1], ALU.add))
                dve.tensor_tensor(cum[1 - par], cum[par], both[par], ALU.add).then_inc(picked, 1)

            FIRST_STEPS = 1 + 4 * TOP_K + 1 + 2

            def route_second(j, par):
                dve.wait_ge(places_free, j + 1)
                dve.wait_ge(rank_done, j + 1)
                dve.tensor_tensor(rank, bank(0)[:, P:P + EXPERTS], room_at, ALU.add).then_inc(ranks_read, 1)
                dve.wait_ge(ranks_read, j + 2)
                own.then_next(dve.tensor_tensor(ranked, picks[par],
                                                rank.unsqueeze(1).to_broadcast([P, TOP_K, EXPERTS]), ALU.mult))
                own.then_next(dve.tensor_reduce(posf, ranked, AX.X, ALU.add))
                own.then_next(dve.tensor_copy(pos[par], posf))
                own.then_next(dve.tensor_copy(meta_i[par][:, :, 1], token.to_broadcast([P, TOP_K])))
                dve.wait_ge(ratio_ready, j + 1)
                own.then_next(dve.tensor_scalar(low, ratio[par], 1.0, None, ALU.add))
                own.then_next(dve.reciprocal(meta[par][:, 0, 0:1], low))
                own.then_next(dve.tensor_tensor(meta[par][:, 1, 0:1], ratio[par], meta[par][:, 0, 0:1], ALU.mult))
                dve.tensor_scalar(token, token, float(P), None, ALU.add).then_inc(pos_ready, 1)
                dve.wait_ge(pos_ready, j + 1)

            SECOND_STEPS = 4 + 3

            def second_norm(j, h, par):
                dve.wait_ge(o_done, j + 1)
                dve.tensor_tensor(tile_of(j), bank(7), tile_of(j), ALU.add).then_inc(res2, 1)
                dve.wait_ge(res2, j + 1)
                if not isinstance(j, int) or j >= 2:
                    dve.wait_ge(x_out[par], h * 16)
                normalize(xr[par], tile_of(j)).then_inc(xn2_ready, 1)

            def low_xn(j, par):
                dve.wait_ge(xn_high_ready, j + 1)
                dve.tensor_tensor(xn_parts[:, par, 1, :, :], xnT[par], xn_parts[:, par, 0, :, :].bitcast(F32),
                                  ALU.subtract).then_inc(xn_parts_ready, 1)

            def low_vo(n):
                dve.wait_ge(vo_high_ready, n + 1)
                dve.tensor_tensor(vo_low[:, n, :], vo_raw[:, n, :], vo_high[:, n, :].bitcast(F32), ALU.subtract
                                  ).then_inc(vo_ready, 1)

            def tile_step(j, h, par, front, back, back2, late=False):
                tops(j, par)
                probs(j, par)
                if not isinstance(j, int) or j + 1 < TILES:
                    low_xn(j + 1, 1 - par)
                copy_pt(j)
                if front:
                    first_norm(j + 2, par)
                copy_ct(j)
                if back2:
                    route_second(j - 2, par)
                if late:
                    second_norm(j, h, par)
                if back:
                    route_first(j - 1, 1 - par)
                if not late:
                    second_norm(j, h, par)

            dve.memset(small[:, 28:29], 0.0).then_inc(ranks_read, 1)
            own.then_next(dve.memset(cum[0], 0.0))
            own.then_next(dve.tensor_copy(token, me))
            first_norm(0, 0)
            first_norm(1, 1)
            low_xn(0, 0)
            low_vo(0)
            attended(TILES - 1, 1)
            for part in range(3 + NEWTON):
                attended_norm(part)
            low_vo(1)
            tile_step(0, 0, 0, True, False, False)
            tile_step(1, 0, 1, True, True, False)
            with dve.Fori(1, TILES // 2 - 1) as h:
                own.enter(h - 1, 2 * (2 + 1 + 1 + 2 * NORM + FIRST_STEPS + SECOND_STEPS))
                for par in range(2):
                    tile_step(h * 2 + par, h, par, True, True, True)
                own.leave(TILES // 2 - 2)
            for j in range(TILES - 2, TILES):
                tile_step(j, j // 2, j % 2, False, True, True, late=(j == TILES - 2))
            route_second(TILES - 2, 0)
            route_first(TILES - 1, 1)

            def split_low(e, b):
                dve.wait_ge(w_high_ready, e * WB + (b + 1))
                dve.tensor_tensor(w_low[:, b, :], w_raw[b], w_high[b].bitcast(F32), ALU.subtract).then_inc(w_ready, 1)

            def low_x(i, par):
                dve.wait_ge(x_high_ready, i + 1)
                dve.tensor_tensor(xT_parts[par][1], bank(7).rearrange("p (k t) -> p k t", k=KC),
                                  xT_parts[par][0].bitcast(F32), ALU.subtract).then_inc(x_ready, 1)

            route_second(TILES - 1, 1)
            split_low(0, 0)
            split_low(0, 1)
            split_low(0, 2)
            low_x(0, 0)

            dve.wait_ge(count_done, 1)
            own.then_next(dve.tensor_scalar(cnt_i, bank(6)[:, 0:EXPERTS], float(P - 1), None, ALU.add))
            own.then_next(dve.tensor_scalar(cnt_r, cnt_i, 7, None, ALU.logical_shift_right))
            own.then_next(dve.tensor_scalar(lots, cnt_r, 1.0, None, ALU.max))
            own.then_next(dve.memset(ends[:, 0:1], 0.0))
            for e in range(EXPERTS):
                own.then_next(dve.tensor_tensor(ends[:, e + 1:e + 2], ends[:, e:e + 1], lots[:, e:e + 1], ALU.add))
            own.then_next(dve.tensor_copy(used, ends[:, EXPERTS:EXPERTS + 1]))
            wide = [P, SLOTS, EXPERTS]
            own.then_next(dve.tensor_tensor(past, slot_no, ends[:, 1:].unsqueeze(1).to_broadcast(wide), ALU.is_ge))
            own.then_next(dve.tensor_reduce(before_f, past, AX.X, ALU.add))
            own.then_next(dve.tensor_tensor(weighed, past, lots.unsqueeze(1).to_broadcast(wide), ALU.mult))
            own.then_next(dve.tensor_reduce(taken, weighed, AX.X, ALU.add))
            own.then_next(dve.tensor_scalar(slot_e, before_f, float(EXPERTS - 1), None, ALU.min))
            own.then_next(dve.scalar_tensor_tensor(out=slot_f, in0=before_f, scalar=float(ROOM), in1=slot_no[:, :, 0],
                                                   op0=ALU.mult, op1=ALU.add))
            own.then_next(dve.tensor_tensor(slot_f, slot_f, taken, ALU.subtract))
            dve.tensor_scalar(slot_at, slot_f, float(PLACES - 1), float(P), ALU.min, ALU.mult).then_inc(slot_ready, 1)

            def low_h(i, f):
                dve.wait_ge(h_high_ready, i * FB + (f + 1))
                chunks = slice(4 * f, 4 * f + 4)
                dve.tensor_tensor(h_parts[:, 1, chunks, :], bank(3 + f % 2).rearrange("p (c t) -> p c t", c=4),
                                  h_parts[:, 0, chunks, :].bitcast(F32), ALU.subtract).then_inc(h_ready, 1)

            def copy_y(i, h, par):
                dve.wait_ge(down_done, i * FB + FB)
                if not isinstance(i, int) or i >= 2:
                    dve.wait_ge(added[par], h * 16)
                dve.wait_ge(gate_ready, i + 1)
                dve.tensor_scalar(yb[par], bank(5 + par), gm[par][:, 0:1], None, ALU.mult).then_inc(y_ready, 1)

            def expert(i):
                return dve.value_load(slot_e[0:1, bass.ds(i, 1)], min_val=0, max_val=EXPERTS - 1)

            def slot(i, h, par, last=False):
                static = isinstance(i, int)
                e = 0 if static and i == 0 else expert(i)
                first = None if static and i == 0 else (e > expert(i - 1))
                after = None if last else expert(i + 1)

                def if_first(b):
                    if first is None:
                        split_low(e, b)
                    else:
                        with dve.If(first):
                            split_low(e, b)

                def if_after(*blocks):
                    if not last:
                        with dve.If(after > e):
                            for b in blocks:
                                split_low(after, b)

                if_first(5)
                low_h(i, 0)
                if_first(6)
                low_h(i, 1)
                if_first(7)
                if_after(0)
                low_h(i, 2)
                if_after(1)
                low_h(i, 3)
                if not last:
                    low_x(i + 1, 1 - par)
                if_after(2, 3, 4)
                copy_y(i, h, par)

            dve.wait_ge(slot_ready, 1)
            split_low(0, 3)
            split_low(0, 4)
            slot(0, 0, 0)
            slot(1, 0, 1)
            slots_in_use = in_use(dve)
            with dve.Fori(1, SLOTS // 2) as h:
                for par in range(2):
                    with dve.If(slots_in_use > h * 2 + par):
                        slot(h * 2 + par, h, par)
            with dve.If(slots_in_use > SLOTS - 1):
                slot(SLOTS - 1, SLOTS // 2, 0, last=True)


def kernel(x, ctx_1024, mask_BxSxS2_ik1, L0_xattn_gamma, L0_xattn_beta, L0_attn_W_qkv, L0_attn_W_out,
           L0_ffn_router_w, L0_ffn_expert_w1, L0_ffn_expert_w2):
    import numpy as np
    import concourse.bacc as bacc
    from concourse.bass_utils import run_bass_kernel_spmd

    c = np.zeros((P, C_END), np.float32)
    c[:, C_ID:C_ID + P] = np.eye(P)
    c[:, C_TRI:C_TRI + P] = np.triu(np.ones((P, P)), 1)
    c[:, C_ONE:C_ONE + P] = 1.0
    c[:, C_ME] = np.arange(P)
    c[:, C_SPARE] = TOKENS + np.arange(P)
    c[:, C_EXP:C_ROOM] = np.arange(EXPERTS) - EXPERTS
    c[:, C_ROOM:C_SLOT] = np.arange(EXPERTS) * TOKENS
    c[:, C_SLOT:C_END] = np.repeat(np.arange(SLOTS), EXPERTS)
    a = {
        "x": np.asarray(x).reshape(TILES * P, D),
        "ctx": np.asarray(ctx_1024),
        "ctx_turned": np.asarray(ctx_1024)[:, :LOADED_TURNED * BLK, :].reshape(BATCH, LOADED_TURNED, BLK, KC, P)
        .transpose(0, 4, 1, 3, 2)[:, :, ::-1],
        "mask": np.asarray(mask_BxSxS2_ik1).reshape(TILES * P, T),
        "gamma": np.asarray(L0_xattn_gamma),
        "beta": np.asarray(L0_xattn_beta),
        "w_qkv": np.asarray(L0_attn_W_qkv).reshape(D, 3, KC, P).transpose(3, 1, 2, 0).reshape(P, -1),
        "w_out": np.asarray(L0_attn_W_out).reshape(D, KC, P).transpose(2, 1, 0).reshape(P, -1),
        "w_router": np.asarray(L0_ffn_router_w).reshape(EXPERTS, KC, P).transpose(2, 1, 0).reshape(P, -1),
        "w1": np.asarray(L0_ffn_expert_w1).reshape(EXPERTS, FB, BLK, KC, P).transpose(0, 4, 1, 3, 2)
        .reshape(EXPERTS, P, -1),
        "w2": np.asarray(L0_ffn_expert_w2).reshape(EXPERTS, D, FC, P).transpose(0, 3, 2, 1).reshape(EXPERTS, P, -1),
        "consts": c,
    }
    a = {f"in_{k}": np.ascontiguousarray(v) for k, v in a.items()}
    nc = bacc.Bacc("TRN2", target_bir_lowering=False, num_devices=1)
    args = [nc.dram_tensor(k, v.shape, mybir.dt.from_np(v.dtype), kind="ExternalInput").ap() for k, v in a.items()]
    out = nc.dram_tensor("out_0", (TOKENS + P, D), F32, kind="ExternalOutput").ap()
    build(nc, *args, out)
    r = run_bass_kernel_spmd(nc, [a], core_ids=[0])
    return np.asarray(r.results[0]["out_0"])[:TOKENS].reshape(BATCH, SEQ, D)
```
